# Optimizing a Trainium2 kernel written in Bass

```python
import numpy as np
import jax
import jax.numpy as jnp

def _softmax(x, axis=-1):
    return jax.nn.softmax(x, axis=axis)

def _gelu(x):
    return jax.nn.gelu(x, approximate=True)

def _silu(x):
    return jax.nn.silu(x)

def _sigmoid(x):
    return jax.nn.sigmoid(x)

def _layernorm(x, axis=-1, eps=1e-05):
    m = jnp.mean(x, axis=axis, keepdims=True)
    v = jnp.var(x, axis=axis, keepdims=True)
    return (x - m) / jnp.sqrt(v + eps)

def _scatter_add(tgt, idx, src, axis=0):
    return tgt.at[idx].add(src)

def _segment_sum(src, seg, n):
    return jax.ops.segment_sum(src, seg, n)
kernel_name = 'mk_flamingo_gated_d1_seqx_r4_f1eb8e'

def setup_inputs(seed: int=0):
    np.random.seed(seed)
    _w = jnp.asarray

    def _rec_inputs():
        import jax
        import jax.numpy as jnp
        _rk = jax.random.key(seed)
        x = -0.0002928 + 1 * jax.random.normal(jax.random.fold_in(_rk, 1), (4, 1024, 256), jnp.float32)
        _lenS = 1024 - jax.random.randint(jax.random.fold_in(_rk, 7), (4,), 0, max(1, 1024 // 4) + 1, jnp.int32)
        _lenS2 = 77 - jax.random.randint(jax.random.fold_in(_rk, 8), (4,), 0, max(1, 77 // 4) + 1, jnp.int32)
        _ctx_1024P = jax.random.normal(jax.random.fold_in(_rk, 11), (4, 16, 256), jnp.float32)
        _ctx_1024c = jax.random.dirichlet(jax.random.fold_in(_rk, 511), 0.3 * jnp.ones((16,), jnp.float32), (4, 77))
        _ctx_1024t = jnp.einsum('bsk,bkd->bsd', _ctx_1024c, _ctx_1024P)
        _ctx_1024t = _ctx_1024t * jax.lax.rsqrt(jnp.mean(jnp.square(_ctx_1024t)) + 1e-12) * 0.953939
        ctx_1024 = -1.39393e-06 + 0.999914 * (_ctx_1024t + 0.3 * jax.random.normal(jax.random.fold_in(_rk, 611), (4, 77, 256), jnp.float32))
        _validS = jnp.arange(1024)[None, :] < _lenS[:, None]
        _validS2 = jnp.arange(77)[None, :] < _lenS2[:, None]
        _causal = jnp.tril(jnp.ones((1024, 1024), dtype=bool))
        mask_Bx1xSxS2_if1 = jnp.where(jnp.ones((4, 1, 1024, 77), dtype=bool), 1, 0).astype(jnp.int32)
        _g = jax.random.normal(jax.random.fold_in(_rk, 9001), (2, 1), jnp.float32)
        _g = jnp.sign(_g) * jnp.maximum(jnp.abs(_g), 1.0) + (_g == 0) * 1.0
        g_xattn = _g[0]
        g_ffn = _g[1]
        return (x, ctx_1024, mask_Bx1xSxS2_if1, g_xattn, g_ffn)
    x, ctx_1024, mask_Bx1xSxS2_if1, g_xattn, g_ffn = _rec_inputs()

    def _L0_xattn_setup():
        import jax, jax.numpy as jnp
        import numpy as np
        HIDDEN = 256
        N_HEAD = 16
        D_HEAD = HIDDEN // N_HEAD
        key = jax.random.key(seed)
        ks = jax.random.split(key, 12)
        B, S, H = (2, 512, HIDDEN)
        scale = 1.0 / np.sqrt(H)
        inp = {'q': jax.random.normal(ks[0], (B, S, H), jnp.float32), 'k': jax.random.normal(ks[1], (B, S, H), jnp.float32), 'v': jax.random.normal(ks[2], (B, S, H), jnp.float32), 'mask': jnp.ones((B, 1, S, S), jnp.int32), 'w_q': jax.random.normal(ks[3], (H, H), jnp.float32) * scale, 'b_q': jnp.zeros((H,), jnp.float32), 'w_k': jax.random.normal(ks[4], (H, H), jnp.float32) * scale, 'b_k': jnp.zeros((H,), jnp.float32), 'w_v': jax.random.normal(ks[5], (H, H), jnp.float32) * scale, 'b_v': jnp.zeros((H,), jnp.float32), 'w_o': jax.random.normal(ks[6], (H, H), jnp.float32) * scale, 'b_o': jnp.zeros((H,), jnp.float32)}
        return inp
    _L0_xattn_all = _L0_xattn_setup()
    _L0_xattn_in = {k: v for k, v in _L0_xattn_all.items() if k in ('w_q', 'b_q', 'w_k', 'b_k', 'w_v', 'b_v', 'w_o', 'b_o')}
    del _L0_xattn_all

    def _L0_ffn_setup():
        import jax, jax.numpy as jnp
        import numpy as np
        B, S, H, I, E, K = (4, 512, 256, 688, 4, 2)
        key = jax.random.key(seed)
        ks = jax.random.split(key, 8)
        inv_h = 1.0 / np.sqrt(H)
        inv_i = 1.0 / np.sqrt(I)
        return {'x': jax.random.normal(ks[0], (B, S, H), jnp.float32), 'gate_w': jax.random.normal(ks[1], (E, H), jnp.float32) * inv_h, 'eg': jax.random.normal(ks[2], (E, I, H), jnp.float32) * inv_h, 'eu': jax.random.normal(ks[3], (E, I, H), jnp.float32) * inv_h, 'ed': jax.random.normal(ks[4], (E, H, I), jnp.float32) * inv_i, 'sg': jax.random.normal(ks[5], (I, H), jnp.float32) * inv_h, 'su': jax.random.normal(ks[6], (I, H), jnp.float32) * inv_h, 'sd': jax.random.normal(ks[7], (H, I), jnp.float32) * inv_i}
    _L0_ffn_all = _L0_ffn_setup()
    _L0_ffn_in = {k: v for k, v in _L0_ffn_all.items() if k in ('gate_w', 'eg', 'eu', 'ed', 'sg', 'su', 'sd')}
    del _L0_ffn_all
    return {'x': x, 'ctx_1024': ctx_1024, 'mask_Bx1xSxS2_if1': mask_Bx1xSxS2_if1, 'g_xattn': g_xattn, 'g_ffn': g_ffn, 'L0_xattn_w_q': _L0_xattn_in['w_q'], 'L0_xattn_b_q': _L0_xattn_in['b_q'], 'L0_xattn_w_k': _L0_xattn_in['w_k'], 'L0_xattn_b_k': _L0_xattn_in['b_k'], 'L0_xattn_w_v': _L0_xattn_in['w_v'], 'L0_xattn_b_v': _L0_xattn_in['b_v'], 'L0_xattn_w_o': _L0_xattn_in['w_o'], 'L0_xattn_b_o': _L0_xattn_in['b_o'], 'L0_ffn_gate_w': _L0_ffn_in['gate_w'], 'L0_ffn_eg': _L0_ffn_in['eg'], 'L0_ffn_eu': _L0_ffn_in['eu'], 'L0_ffn_ed': _L0_ffn_in['ed'], 'L0_ffn_sg': _L0_ffn_in['sg'], 'L0_ffn_su': _L0_ffn_in['su'], 'L0_ffn_sd': _L0_ffn_in['sd']}

def reference(x, ctx_1024, mask_Bx1xSxS2_if1, g_xattn, g_ffn, L0_xattn_w_q, L0_xattn_b_q, L0_xattn_w_k, L0_xattn_b_k, L0_xattn_w_v, L0_xattn_b_v, L0_xattn_w_o, L0_xattn_b_o, L0_ffn_gate_w, L0_ffn_eg, L0_ffn_eu, L0_ffn_ed, L0_ffn_sg, L0_ffn_su, L0_ffn_sd):
    import jax
    import jax.numpy as jnp

    def _L0_xattn_ref(q, k, v, mask, w_q, b_q, w_k, b_k, w_v, b_v, w_o, b_o):
        import jax, jax.numpy as jnp
        import numpy as np
        HIDDEN = 256
        N_HEAD = 16
        D_HEAD = HIDDEN // N_HEAD
        B, Sq, H = q.shape
        Sk = k.shape[1]
        qh = (q @ w_q + b_q).reshape(B, Sq, N_HEAD, D_HEAD).transpose(0, 2, 1, 3)
        kh = (k @ w_k + b_k).reshape(B, Sk, N_HEAD, D_HEAD).transpose(0, 2, 1, 3)
        vh = (v @ w_v + b_v).reshape(B, Sk, N_HEAD, D_HEAD).transpose(0, 2, 1, 3)
        scores = jnp.einsum('bhqd,bhkd->bhqk', qh, kh) * D_HEAD ** (-0.5)
        scores = jnp.where(mask == 0, jnp.float32(-10000.0), scores)
        attn = jax.nn.softmax(scores, axis=-1)
        out = jnp.einsum('bhqk,bhkd->bhqd', attn, vh)
        out = out.transpose(0, 2, 1, 3).reshape(B, Sq, H)
        return out @ w_o + b_o

    def _L0_ffn_ref(x, gate_w, eg, eu, ed, sg, su, sd):
        import jax, jax.numpy as jnp
        import numpy as np
        B, S, H, I, E, K = (4, 512, 256, 688, 4, 2)
        xf = x.reshape(-1, x.shape[-1])
        scores = jax.nn.softmax(xf @ gate_w.T, axis=-1)
        topk_w, topk_idx = jax.lax.top_k(scores, K)
        topk_w = topk_w / (topk_w.sum(axis=-1, keepdims=True) + 1e-20)
        comb = jnp.sum(jax.nn.one_hot(topk_idx, E, dtype=x.dtype) * topk_w[..., None], axis=1)
        g = jax.nn.silu(jnp.einsum('nh,eih->eni', xf, eg))
        u = jnp.einsum('nh,eih->eni', xf, eu)
        y_exp = jnp.einsum('eni,ehi->enh', g * u, ed)
        y = jnp.einsum('enh,ne->nh', y_exp, comb)
        y = y + jax.nn.silu(xf @ sg.T) * (xf @ su.T) @ sd.T
        return y.reshape(x.shape)
    x = x + jnp.tanh(g_xattn[0]) * _L0_xattn_ref(_layernorm(x, axis=-1), ctx_1024, ctx_1024, mask_Bx1xSxS2_if1, L0_xattn_w_q, L0_xattn_b_q, L0_xattn_w_k, L0_xattn_b_k, L0_xattn_w_v, L0_xattn_b_v, L0_xattn_w_o, L0_xattn_b_o)
    x = x + jnp.tanh(g_ffn[0]) * _L0_ffn_ref(_layernorm(x, axis=-1), L0_ffn_gate_w, L0_ffn_eg, L0_ffn_eu, L0_ffn_ed, L0_ffn_sg, L0_ffn_su, L0_ffn_sd)
    return x

_drawn_inputs = setup_inputs


def setup_inputs(seed=0):
    import zlib

    import numpy as np

    out = dict(_drawn_inputs(seed))
    spreads = {'L0_xattn_b_q': (0.0, 0.1),
     'L0_xattn_b_k': (0.0, 0.1),
     'L0_xattn_b_v': (0.0, 0.1),
     'L0_xattn_b_o': (0.0, 0.1)}
    factors = {}
    for name, (base, spread) in spreads.items():
        noise = np.random.default_rng([zlib.crc32(name.encode()), seed]).standard_normal(out[name].shape)
        drawn = base * np.exp(spread * noise) if base else spread * noise
        out[name] = jnp.asarray(drawn.astype(out[name].dtype))
    for name, factor in factors.items():
        out[name] = (out[name] * factor).astype(out[name].dtype)
    return out
```

```python
import concourse.bass as bass
from concourse import mybir
from contextlib import ExitStack

fp32 = mybir.dt.float32
f32r = mybir.dt.float32r
i32 = mybir.dt.int32
u8 = mybir.dt.uint8
ALU = mybir.AluOpType
ACT = mybir.ActivationFunctionType
AX = mybir.AxisListType

P = 128
B, S, H = 4, 1024, 256
SK = 77
NH, DH = 16, 16
N = B * S
NT = N // P
UT = 2
NU = NT // UT
UB = NU // B
KC = H // P
HH = NH // 2
HW = HH * SK
CH = 5
PW = CH * P
E = 4
EPS = 1e-5
TOPK = 2
PUTS = 8
FF = 688
FC = -(-FF // P)
FH = FF // 2
NS = NT * TOPK + E
PASSES = ((0, 0), (0, 1), (1, 0))


def flamingo(nc, x, ctx_in, mask, g_x, g_f, w_q, b_q, w_k, b_k, w_v, b_v, w_o, b_o,
             gate_w, eg, eu, ed, sg, su, sd, out):
    xf = x.rearrange("b s h -> (b s) h")
    x1_d = nc.dram_tensor("x1_scratch", (N, H), fp32, kind="Internal").ap()
    xn_d = nc.dram_tensor("xn_scratch", (N + P, H), fp32, kind="Internal").ap()
    slots_d = nc.dram_tensor("slots_scratch", (NS * P, 2), fp32, kind="Internal").ap()
    top = ExitStack()
    with top:
        def allocator(stack):
            def sb(name, shape, dt=fp32):
                return stack.enter_context(nc.sbuf_tensor(name, shape, dt))

            def ps(name, shape, dt=fp32):
                return stack.enter_context(nc.psum_tensor(name, shape, dt))

            def sem(name):
                return stack.enter_context(nc.semaphore(name))
            return sb, ps, sem

        sb, ps, sem = allocator(top)
        ident = sb("ident", [P, P])
        tgx = sb("tgx", [P, 1])
        tgf = sb("tgf", [P, 1])
        lg = sb("lg", [P, NT, E])

        attn = ExitStack()
        with attn:
            asb, aps, asem = allocator(attn)
            kblk = [asb(f"kblk_{s}", [P, B, KC * HW], f32r) for s in ("hi", "lo")]
            vp = [asb(f"vp_{s}", [P, B * KC * CH, H], f32r) for s in ("hi", "lo")]
            wq = [asb(f"wq_{s}", [P, KC, H], f32r) for s in ("hi", "lo")]
            gwT = asb("gwT", [P, KC, E])
            xall = asb("xall", [P, NT, H])
            bq = asb("bq", [P, KC])
            bog = asb("bog", [P, H])
            s_x0 = asem("s_x0")
            s_x = asem("s_x")
            prepare_attention(nc, allocator, locals())
            attention(nc, allocator, locals())

        wgu = [sb(f"wgu_{s}", [P, (E + 1) * KC, 2 * FF], f32r) for s in ("hi", "lo")]
        wd = [sb(f"wd_{s}", [P, (E + 1) * FC, H], f32r) for s in ("hi", "lo")]
        slot_of = sb("slot_of", [P, TOPK, NT], i32)
        entry = sb("entry", [P, TOPK, NT, 2])
        expert_of = sb("expert_of", [1, NS], i32)
        slots = sb("slots", [P, NS, 2])
        route_and_prepare(nc, allocator, locals())
        feed_forward(nc, allocator, locals())


def prepare_attention(nc, allocator, v):
    ident, tgx, tgf, kblk, vp, wq, gwT, xall, bq, bog = (v[k] for k in (
        "ident", "tgx", "tgf", "kblk", "vp", "wq", "gwT", "xall", "bq", "bog"))
    s_x0, s_x = v["s_x0"], v["s_x"]
    st = ExitStack()
    with st:
        sb, ps, sem = allocator(st)
        ctx_sb = sb("ctx_sb", [SK, B, H])
        ctxT = sb("ctxT", [P, KC, B * SK])
        wraw = {n: sb(f"{n}_raw", [P, KC, H]) for n in ("wq", "wk", "wv", "wo")}
        wo = [sb(f"wo_{s}", [P, KC, H], f32r) for s in ("hi", "lo")]
        gw_sb = sb("gw_sb", [E, H])
        bkv = sb("bkv", [P, 2, KC])
        kv = sb("kv", [P, 2, KC, B * SK])
        kv_s = [sb(f"kv_{s}", [P, 2, KC, B * SK], f32r) for s in ("hi", "lo")]
        vblkT = [sb(f"vblkT_{s}", [P, KC, HW], f32r) for s in ("hi", "lo")]
        own = sb("own", [P, HH])
        p_ctx = [ps(f"p_ctx{k}", [P, 512]) for k in range(KC)]
        p_kv = [ps(f"p_kv{k}", [P, 512]) for k in range(2 * KC)]
        p_vp = [ps(f"p_vp{k}", [P, 512]) for k in range(2)]
        s_ctx, s_w, s_small, s_gw = sem("s_ctx"), sem("s_w"), sem("s_small"), sem("s_gw")
        s_id, s_own = sem("s_id"), sem("s_own")
        s_ctxps, s_ctxT, s_kvps, s_kv, s_kvhi, s_kvlo = (sem(n) for n in (
            "s_ctxps", "s_ctxT", "s_kvps", "s_kv", "s_kvhi", "s_kvlo"))
        s_wqhi, s_wqlo, s_wohi, s_wolo = (sem(n) for n in ("s_wqhi", "s_wqlo", "s_wohi", "s_wolo"))
        s_tg, s_blkhi = sem("s_tg"), sem("s_blkhi")
        s_blk, s_vps, s_vphi, s_vplo, s_gwps, s_bog = (sem(n) for n in (
            "s_blk", "s_vps", "s_vphi", "s_vplo", "s_gwps", "s_bog"))
        block = st.enter_context(nc.Block())

        xt = v["xf"].rearrange("(t p) d -> p t d", p=P)

        @block.sync
        def _(sp):
            sp.dma_start(ctx_sb[:, :, :], v["ctx_in"].rearrange("b k d -> k b d")).then_inc(s_ctx, 16)
            for n in ("wk", "wv", "wo", "wq"):
                src = v["w_" + n[1]]
                sp.dma_start(wraw[n][:, :, :], src.rearrange("(c p) d -> p c d", p=P)).then_inc(s_w, 16)
            sp.dma_start(xall[:, 0:UT, :], xt[:, 0:UT, :]).then_inc(s_x0, 16)
            sp.dma_start(xall[:, UT:NT, :], xt[:, UT:NT, :]).then_inc(s_x, 16)

        @block.gpsimd
        def _(pool):
            pool.memset(ident[:, :], 0.0).then_inc(s_id, 1)
            pool.memset(own[:, :], 1.0).then_inc(s_own, 1)
            pool.wait_ge(s_id, 1)
            pool.affine_select(out=ident[:, :], in_=ident[:, :], compare_op=ALU.not_equal, fill=1.0,
                               base=0, pattern=[[-1, P]], channel_multiplier=1).then_inc(s_id, 1)
            pool.wait_ge(s_own, 1)
            pool.affine_select(out=own[:, :], in_=own[:, :], compare_op=ALU.is_ge, fill=0.0,
                               base=0, pattern=[[-DH, HH]], channel_multiplier=1).then_inc(s_own, 1)
            pool.wait_ge(s_own, 2)
            pool.affine_select(out=own[:, :], in_=own[:, :], compare_op=ALU.is_ge, fill=0.0,
                               base=DH - 1, pattern=[[DH, HH]], channel_multiplier=-1).then_inc(s_own, 1)
            pool.wait_ge(s_own, 3)
            pool.wait_ge(s_kvlo, 1)
            for b in range(B):
                for m in range(KC):
                    for j, dst in ((0, kblk[1][:, b, m * HW:(m + 1) * HW]), (1, vblkT[1][:, m, :])):
                        if j == 1 and b >= 1:
                            pool.wait_ge(s_vps, 2 * CH * (b - 1) + CH * (m + 1))
                        src = kv_s[1][:, j, m, b * SK:(b + 1) * SK]
                        pool.tensor_tensor(
                            dst.rearrange("p (h k) -> p h k", h=HH),
                            src.unsqueeze(1).broadcast_to([P, HH, SK]),
                            own[:, :].unsqueeze(2).broadcast_to([P, HH, SK]), ALU.mult).then_inc(s_blk, 1)

        @block.scalar
        def _(act):
            act.dma_start(bq[:, :], v["b_q"].rearrange("(c p) -> p c", p=P), allow_slow_non_contiguous=True).then_inc(s_small, 16)
            act.dma_start(bkv[:, 0, :], v["b_k"].rearrange("(c p) -> p c", p=P), allow_slow_non_contiguous=True).then_inc(s_small, 16)
            act.dma_start(bkv[:, 1, :], v["b_v"].rearrange("(c p) -> p c", p=P), allow_slow_non_contiguous=True).then_inc(s_small, 16)
            act.dma_start(bog[:, :], v["b_o"].partition_broadcast(P)).then_inc(s_small, 16)
            act.dma_start(tgx[:, :], v["g_x"].partition_broadcast(P), allow_slow_non_contiguous=True).then_inc(s_small, 16)
            act.dma_start(tgf[:, :], v["g_f"].partition_broadcast(P), allow_slow_non_contiguous=True).then_inc(s_small, 16)
            act.dma_start(gw_sb[:, :], v["gate_w"]).then_inc(s_small, 16)
            act.wait_ge(s_small, 112)
            act.activation(tgx[:, :], tgx[:, :], ACT.Tanh).then_inc(s_tg, 1)
            act.activation(tgf[:, :], tgf[:, :], ACT.Tanh).then_inc(s_tg, 1)
            act.wait_ge(s_w, 64)
            act.activation(wq[0][:, :, :], wraw["wq"][:, :, :], ACT.Copy).then_inc(s_wqhi, 1)
            act.activation(wo[0][:, :, :], wraw["wo"][:, :, :], ACT.Copy).then_inc(s_wohi, 1)
            act.wait_ge(s_kv, 4)
            act.activation(kv_s[0][:, :, :, :], kv[:, :, :, :], ACT.Copy).then_inc(s_kvhi, 1)
            for n in range(B * KC * CH):
                act.wait_ge(s_vps, n + 1)
                rows = HW - 4 * P if n % CH == CH - 1 else P
                act.activation(vp[0][0:rows, n, :], p_vp[n % 2][0:rows, 0:H], ACT.Copy).then_inc(s_vphi, 1)

        @block.vector
        def _(dve):
            dve.wait_ge(s_ctxps, 1)
            for k in range(KC):
                nc.vector.tensor_copy(ctxT[:, k, :], p_ctx[k][:, 0:B * SK]).then_inc(s_ctxT, 1)
            nc.vector.tensor_copy(gwT[:, :, :], p_vp[1][:, 0:KC * E].rearrange("p (c e) -> p c e", e=E)).then_inc(s_ctxT, 1)
            dve.wait_ge(s_small, 112)
            for j in range(2):
                for m in range(KC):
                    dve.wait_ge(s_kvps, 2 * j + m + 1)
                    nc.vector.tensor_scalar(kv[:, j, m, :], p_kv[2 * j + m][:, 0:B * SK], bkv[:, j, m:m + 1],
                                            DH ** -0.5 if j == 0 else 1.0, ALU.add, ALU.mult).then_inc(s_kv, 1)
            dve.wait_ge(s_kv, 4)
            dve.wait_ge(s_kvhi, 1)
            nc.vector.tensor_tensor(kv_s[1][:, :, :, :], kv[:, :, :, :], kv_s[0][:, :, :, :],
                                    ALU.subtract).then_inc(s_kvlo, 1)
            dve.wait_ge(s_wohi, 1)
            nc.vector.tensor_tensor(wo[1][:, :, :], wraw["wo"][:, :, :], wo[0][:, :, :], ALU.subtract).then_inc(s_wolo, 1)
            dve.wait_ge(s_own, 3)
            blk_done = 0
            for b in range(B):
                for m in range(KC):
                    for j, dst in ((1, vblkT[0][:, m, :]), (0, kblk[0][:, b, m * HW:(m + 1) * HW])):
                        if j == 1 and b >= 1:
                            dve.wait_ge(s_vps, 2 * CH * (b - 1) + CH * (m + 1))
                        src = kv_s[0][:, j, m, b * SK:(b + 1) * SK]
                        ins = nc.vector.tensor_tensor(
                            dst.rearrange("p (h k) -> p h k", h=HH),
                            src.unsqueeze(1).broadcast_to([P, HH, SK]),
                            own[:, :].unsqueeze(2).broadcast_to([P, HH, SK]), ALU.mult)
                        if j == 1:
                            ins.then_inc(s_blkhi, 1)
                    for c in range(CH):
                        n = (b * KC + m) * CH + c
                        dve.wait_ge(s_vphi, n + 1)
                        rows = HW - 4 * P if c == CH - 1 else P
                        nc.vector.tensor_tensor(vp[1][0:rows, n, :], p_vp[n % 2][0:rows, 0:H], vp[0][0:rows, n, :],
                                                ALU.subtract).then_inc(s_vplo, 1)
            dve.wait_ge(s_wqhi, 1)
            nc.vector.tensor_tensor(wq[1][:, :, :], wraw["wq"][:, :, :], wq[0][:, :, :], ALU.subtract).then_inc(s_wqlo, 1)
            dve.wait_ge(s_tg, 2)
            nc.vector.tensor_scalar(bog[:, :], bog[:, :], tgx[:, :], None, ALU.mult).then_inc(s_bog, 1)

        @block.tensor
        def _(pe):
            pe.wait_ge(s_id, 2)
            pe.wait_ge(s_ctx, 16)
            pe.wait_ge(s_small, 112)
            for b in range(B):
                for k in range(KC):
                    nc.tensor.transpose(p_ctx[k][:, b * SK:(b + 1) * SK], ctx_sb[:, b, k * P:(k + 1) * P],
                                        ident[0:SK, 0:SK])
            for k in range(KC):
                last = nc.tensor.transpose(p_vp[1][:, k * E:(k + 1) * E], gw_sb[:, k * P:(k + 1) * P],
                                           ident[0:E, 0:E])
            last.then_inc(s_ctxps, 1)
            pe.wait_ge(s_w, 64)
            pe.wait_ge(s_ctxT, 3)
            for j, n in enumerate(("wk", "wv")):
                for m in range(KC):
                    for k in range(KC):
                        last = nc.tensor.matmul(p_kv[2 * j + m][:, 0:B * SK], wraw[n][:, k, m * P:(m + 1) * P],
                                                ctxT[:, k, :], start=(k == 0), stop=(k == KC - 1))
                    last.then_inc(s_kvps, 1)
            pe.wait_ge(s_wolo, 1)
            for b in range(B):
                for m in range(KC):
                    pe.wait_ge(s_blkhi, b * KC + m + 1)
                    pe.wait_ge(s_blk, 2 * (b * KC + m + 1))
                    for c in range(CH):
                        n = (b * KC + m) * CH + c
                        rows = HW - 4 * P if c == CH - 1 else P
                        if n >= 2:
                            pe.wait_ge(s_vplo, n - 1)
                        for q, (i, j) in enumerate(((0, 0), (0, 1), (1, 0))):
                            last = nc.tensor.matmul(p_vp[n % 2][0:rows, 0:H], vblkT[i][:, m, c * P:c * P + rows],
                                                    wo[j][:, m, :], start=(q == 0), stop=(q == 2))
                        last.then_inc(s_vps, 1)


def attention(nc, allocator, v):
    ident, tgx, kblk, vp, wq, gwT, xall, bq, bog, lg = (v[k] for k in (
        "ident", "tgx", "kblk", "vp", "wq", "gwT", "xall", "bq", "bog", "lg"))
    s_x0, s_x = v["s_x0"], v["s_x"]
    x1_t = v["x1_d"].rearrange("(t p) d -> p t d", p=P)
    xn_t = v["xn_d"][0:N, :].rearrange("(t p) d -> p t d", p=P)
    st = ExitStack()
    with st:
        sb, ps, sem = allocator(st)
        prob = [sb(f"prob{t}", [P, KC * PW]) for t in range(UT)]
        pT = [sb(f"pT_{s}", [P, KC * CH, P], f32r) for s in ("hi", "lo")]
        xh = sb("xh", [P, UT, H])
        xT = [sb(f"xT_{s}", [P, KC, UT * P], f32r) for s in ("hi", "lo")]
        qT = [sb(f"qT_{s}", [P, KC, UT * P], f32r) for s in ("hi", "lo")]
        xn = sb("xn", [P, UT, H])
        xnT = sb("xnT", [P, KC, UT * P])
        lgs = sb("lgs", [E, UT * P])
        st1 = sb("st1", [P, UT, 6])
        mv1 = sb("mv1", [P, UT, 2])
        rs1 = sb("rs1", [P, UT])
        st2 = sb("st2", [P, UT, 6])
        mv2 = sb("mv2", [P, UT, 2])
        rs2 = sb("rs2", [P, UT])
        negmax = sb("negmax", [P, UT, NH])
        rowsum = sb("rowsum", [P, UT, NH])
        rinv = sb("rinv", [P, UT, NH])
        hidden = sb("hidden", [P, 1])
        mask_in = sb("mask_in", [P, UT, SK], i32)
        blind = sb("blind", [P, UT, SK], i32)
        half = sb("half", [P, UT])
        epst = sb("epst", [P, UT])
        p_s = ps("p_s", [P, 2 * KC, 512])
        p_t = [ps(f"p_t{k}", [P, 512]) for k in range(2)]
        p_o = ps("p_o", [P, 512])
        p_m = ps("p_m", [P, 512])
        names = ("s_mask s_blind s_const s_zero s_ln s_mv1 s_ve1 s_rs1 s_xh s_xT s_xThi s_xTlo s_q s_qhi s_qlo s_S s_cp s_max s_exp s_rec s_P "
                 "s_T s_Thi s_Tlo s_PV s_xb s_x1 s_bn2 s_mv2 s_ve2 s_rs2 s_xn s_xnT s_xnc s_lgT s_lgs s_lg s_lgc s_st").split()
        g = {n: sem(n) for n in names}
        (s_mask, s_blind, s_const, s_zero, s_ln, s_mv1, s_ve1, s_rs1, s_xh, s_xT, s_xThi, s_xTlo, s_q, s_qhi, s_qlo, s_S, s_cp, s_max, s_exp, s_rec,
         s_P, s_T, s_Thi, s_Tlo, s_PV, s_xb, s_x1, s_bn2, s_mv2, s_ve2, s_rs2, s_xn, s_xnT, s_xnc, s_lgT, s_lgs, s_lg,
         s_lgc, s_st) = (g[n] for n in names)
        block = st.enter_context(nc.Block())
        s_turn = {nc.vector: sem("s_turn_dve"), nc.tensor: sem("s_turn_pe")}
        GROUPS = ((0, 4), (4, 4), (8, 2))
        PASSES = ((0, 0), (0, 1), (1, 0))

        def wait(eng, s, val):
            if isinstance(val, int) and val <= 0:
                return
            eng.wait_ge(s, val)

        def settle(eng):
            eng.sem_inc(s_turn[eng], 1)

        def steps(eng, step):
            for i in range(3):
                step(i)
            with eng.Fori(3, NU - 2) as i:
                step(i)
            for i in range(NU - 2, NU + 2):
                step(i)

        def on(i, lag):
            return not isinstance(i, int) or 0 <= i - lag < NU

        mask_t = v["mask"].rearrange("b o (t p) k -> p (b o t) k", p=P)

        @block.sync
        def _(sp):
            def mask_load(n):
                wait(sp, s_blind, n)
                sp.dma_start(mask_in[:, :, :], mask_t[:, bass.ds(UT * n, UT), :]).then_inc(s_mask, 16)

            mask_load(0)

            def step(i):
                if on(i, -1):
                    mask_load(i + 1)
                if on(i, 2):
                    w = i - 2
                    sp.wait_ge(s_xn, w + 1)
                    sp.dma_start(x1_t[:, bass.ds(2 * w, UT), :], xall[:, bass.ds(2 * w, UT), :]).then_inc(s_st, 16)
                    sp.dma_start(xn_t[:, bass.ds(2 * w, UT), :], xn[:, :, :]).then_inc(s_st, 16)
            steps(sp, step)
            sp.wait_ge(s_st, 32 * NU)

        @block.gpsimd
        def _(pool):
            pool.memset(half[:, :], -0.5).then_inc(s_const, 1)
            pool.memset(epst[:, :], EPS).then_inc(s_const, 1)
            pool.wait_ge(s_const, 2)

            def rstd(mv, rs, s_in, s_mid, s_out, n):
                pool.wait_ge(s_in, n)
                pool.tensor_tensor(rs[:, :], mv[:, :, 1], epst[:, :], ALU.add).then_inc(s_mid, 1)
                pool.wait_ge(s_mid, n)
                pool.tensor_tensor(rs[:, :], rs[:, :], half[:, :], ALU.pow).then_inc(s_out, 1)

            def residual_bias(n):
                pool.wait_ge(s_xh, n + 1)
                pool.tensor_tensor(xall[:, bass.ds(2 * n, UT), :], xall[:, bass.ds(2 * n, UT), :],
                                   bog[:, :].unsqueeze(1).broadcast_to([P, UT, H]), ALU.add).then_inc(s_xb, 1)

            rstd(mv1, rs1, s_mv1, s_ve1, s_rs1, 1)
            residual_bias(0)
            rstd(mv1, rs1, s_mv1, s_ve1, s_rs1, 2)

            def step(i):
                if on(i, -1):
                    residual_bias(i + 1)
                if on(i, -2):
                    rstd(mv1, rs1, s_mv1, s_ve1, s_rs1, i + 3)
                if on(i, 0):
                    for t in range(UT):
                        for m in range(KC):
                            pool.wait_ge(s_rec, 4 * i + 2 * t + m + 1)
                            pr = prob[t][:, m * PW:m * PW + HW].rearrange("p (h k) -> p h k", k=SK)
                            pool.tensor_tensor(pr, pr, rinv[:, t, m * HH:(m + 1) * HH].unsqueeze(2).broadcast_to(
                                [P, HH, SK]), ALU.mult).then_inc(s_P, 1)
                if on(i, 1):
                    rstd(mv2, rs2, s_mv2, s_ve2, s_rs2, i)
            steps(pool, step)

        @block.scalar
        def _(act):
            def xT_hi(n):
                act.wait_ge(s_xT, n + 1)
                act.activation(xT[0][:, :, :], p_m[:, :].rearrange("p (c t) -> p c t", c=KC), ACT.Copy).then_inc(s_xThi, 1)

            def q_hi(n):
                act.wait_ge(s_q, n + 1)
                for m in range(KC):
                    ins = act.activation(qT[0][:, m, :], p_m[:, m * UT * P:(m + 1) * UT * P], ACT.Identity,
                                         bias=bq[:, m:m + 1])
                ins.then_inc(s_qhi, 1)

            def t_hi(i, t, gi):
                c0, cn = GROUPS[gi]
                G = 6 * (i - 1) + 3 * t + gi
                act.wait_ge(s_T, G + 1)
                wait(act, s_PV, G - 2)
                act.activation(pT[0][:, c0:c0 + cn, :],
                               p_t[(3 * t + gi) % 2][:, 0:cn * P].rearrange("p (c t) -> p c t", t=P),
                               ACT.Copy).then_inc(s_Thi, 1)

            def exps(i, t, m):
                act.wait_ge(s_max, 4 * i + 2 * t + m + 1)
                wait(act, s_T, 6 * (i - 1) + 3 * t + 2 + m)
                wait(act, s_P, 4 * (i - 1) + 2 * t + m + 1)
                for h in range(HH):
                    hd = m * HH + h
                    col = (h % 4) * SK
                    ins = act.activation(prob[t][:, m * PW + h * SK:m * PW + (h + 1) * SK],
                                         p_s[:, 2 * m + h // 4, col:col + SK], ACT.Exp,
                                         bias=negmax[:, t, hd:hd + 1],
                                         accum_out=rowsum[:, t, hd:hd + 1])
                ins.then_inc(s_exp, 1)

            xT_hi(0)
            q_hi(0)

            def step(i):
                for t in range(UT):
                    if on(i, 1):
                        t_hi(i, t, 0)
                        t_hi(i, t, 1)
                    if t == 1 and on(i, -1):
                        xT_hi(i + 1)
                    if t == 0 and on(i, 2):
                        act.wait_ge(s_xnT, i - 1)
                        act.activation(xnT[:, :, :], p_m[:, :].rearrange("p (c t) -> p c t", c=KC),
                                       ACT.Copy).then_inc(s_xnc, 1)
                    if on(i, 0):
                        exps(i, t, 0)
                    if on(i, 1):
                        t_hi(i, t, 2)
                    if t == 1 and on(i, -1):
                        q_hi(i + 1)
                    if t == 0 and on(i, 2):
                        act.wait_ge(s_lgT, i - 1)
                        act.activation(lgs[:, :], p_m[0:E, 0:UT * P], ACT.Copy).then_inc(s_lgs, 1)
                    if on(i, 0):
                        exps(i, t, 1)
                    if t == 0 and on(i, 2):
                        act.wait_ge(s_lg, i - 1)
                        act.activation(lg[:, bass.ds(2 * (i - 2), UT), :],
                                       p_m[:, 0:UT * E].rearrange("p (t e) -> p t e", t=UT), ACT.Copy).then_inc(s_lgc, 1)
            steps(act, step)

        @block.vector
        def _(dve):
            nc.vector.memset(hidden[:, :], -10000.0)
            for t in range(UT):
                for m in range(KC):
                    ins = nc.vector.memset(prob[t][:, m * PW + HW:(m + 1) * PW], 0.0)
            ins.then_inc(s_zero, 1)
            dve.wait_ge(s_zero, 1)

            def stats(n):
                for t in range(UT):
                    ins = nc.vector.bn_stats(st1[:, t, :], xall[:, bass.ds(2 * n + t, 1), :])
                ins.then_inc(s_ln, 1)
                dve.wait_ge(s_ln, n + 1)
                settle(dve)
                for t in range(UT):
                    ins = nc.vector.bn_aggr(mv1[:, t, :], st1[:, t, :])
                ins.then_inc(s_mv1, 1)

            def normed(n):
                dve.wait_ge(s_rs1, n + 1)
                wait(dve, s_xT, n)
                for t in range(UT):
                    ins = nc.vector.tensor_scalar(xh[:, t, :], xall[:, bass.ds(2 * n + t, 1), :], mv1[:, t, 0:1],
                                                  rs1[:, t:t + 1], ALU.subtract, ALU.mult)
                ins.then_inc(s_xh, 1)

            def xT_lo(n):
                dve.wait_ge(s_xThi, n + 1)
                nc.vector.tensor_tensor(xT[1][:, :, :], p_m[:, :].rearrange("p (c t) -> p c t", c=KC), xT[0][:, :, :],
                                        ALU.subtract).then_inc(s_xTlo, 1)

            def q_lo(n):
                dve.wait_ge(s_qhi, n + 1)
                for m in range(KC):
                    ins = nc.vector.scalar_tensor_tensor(out=qT[1][:, m, :], in0=p_m[:, m * UT * P:(m + 1) * UT * P],
                                                         scalar=bq[:, m:m + 1], in1=qT[0][:, m, :], op0=ALU.add,
                                                         op1=ALU.subtract)
                ins.then_inc(s_qlo, 1)

            def no_sight(n):
                dve.wait_ge(s_mask, 16 * (n + 1))
                nc.vector.tensor_scalar(blind[:, :, :], mask_in[:, :, :], 0.0, None, ALU.is_equal).then_inc(s_blind, 1)

            def half_max(i, t, m):
                dve.wait_ge(s_S, 4 * i + 2 * t + m + 1)
                wait(dve, s_exp, 4 * (i - 1) + 2 * t + m + 1)
                sc = p_s[:, 2 * m:2 * m + 2, 0:4 * SK].rearrange("p n (h k) -> p n h k", k=SK)
                shape = [P, 2, 4, SK]
                dve.wait_ge(s_blind, i + 1)
                settle(dve)
                nc.vector.copy_predicated(
                    sc, blind[:, t, :].unsqueeze(1).unsqueeze(1).broadcast_to(shape),
                    hidden[:, :].unsqueeze(2).unsqueeze(3).broadcast_to(shape)).then_inc(s_cp, 1)
                dve.wait_ge(s_cp, 4 * i + 2 * t + m + 1)
                nc.vector.tensor_reduce(negmax[:, t, m * HH:(m + 1) * HH].rearrange("p (n h) -> p n h", h=4), sc,
                                        AX.X, ALU.max, negate=True).then_inc(s_max, 1)

            def t_lo(i, t, gi):
                c0, cn = GROUPS[gi]
                G = 6 * (i - 1) + 3 * t + gi
                dve.wait_ge(s_Thi, G + 1)
                wait(dve, s_PV, G - 2)
                nc.vector.tensor_tensor(pT[1][:, c0:c0 + cn, :],
                                        p_t[(3 * t + gi) % 2][:, 0:cn * P].rearrange("p (c t) -> p c t", t=P),
                                        pT[0][:, c0:c0 + cn, :], ALU.subtract).then_inc(s_Tlo, 1)

            def recip(i, t, m):
                dve.wait_ge(s_exp, 4 * i + 2 * t + m + 1)
                wait(dve, s_P, 4 * (i - 1) + 2 * t + m + 1)
                nc.vector.reciprocal(rinv[:, t, m * HH:(m + 1) * HH], rowsum[:, t, m * HH:(m + 1) * HH]).then_inc(s_rec, 1)

            dve.wait_ge(s_x0, 16)
            no_sight(0)
            stats(0)
            normed(0)
            xT_lo(0)
            dve.wait_ge(s_x, 16)
            stats(1)
            normed(1)
            q_lo(0)

            def step(i):
                for t in range(UT):
                    if on(i, 0):
                        half_max(i, t, 0)
                    if t == 0 and on(i, 2):
                        w = i - 2
                        dve.wait_ge(s_rs2, w + 1)
                        wait(dve, s_xnT, w)
                        wait(dve, s_st, 32 * w)
                        for tt in range(UT):
                            ins = nc.vector.tensor_scalar(xn[:, tt, :], xall[:, bass.ds(2 * w + tt, 1), :],
                                                          mv2[:, tt, 0:1], rs2[:, tt:tt + 1],
                                                          ALU.subtract, ALU.mult)
                        ins.then_inc(s_xn, 1)
                    if on(i, 1):
                        t_lo(i, t, 0)
                        t_lo(i, t, 1)
                    if t == 0 and on(i, -2):
                        stats(i + 2)
                    if t == 1 and on(i, -1):
                        xT_lo(i + 1)
                    if on(i, 0):
                        half_max(i, t, 1)
                        recip(i, t, 0)
                    if on(i, 1):
                        t_lo(i, t, 2)
                    if t == 1 and on(i, -1):
                        q_lo(i + 1)
                    if on(i, 1):
                        u = i - 1
                        dve.wait_ge(s_PV, 6 * u + 3 * t + 3)
                        wait(dve, s_xb, u + 1)
                        nc.vector.scalar_tensor_tensor(
                            out=xall[:, bass.ds(2 * u + t, 1), :], in0=p_o[:, 0:H], scalar=tgx[:, :],
                            in1=xall[:, bass.ds(2 * u + t, 1), :], op0=ALU.mult, op1=ALU.add).then_inc(s_x1, 1)
                        dve.wait_ge(s_x1, 2 * u + t + 1)
                        settle(dve)
                        nc.vector.bn_stats(st2[:, t, :], xall[:, bass.ds(2 * u + t, 1), :]).then_inc(s_bn2, 1)
                    if on(i, 0):
                        recip(i, t, 1)
                if on(i, 1):
                    dve.wait_ge(s_bn2, 2 * i)
                    settle(dve)
                    for t in range(UT):
                        ins = nc.vector.bn_aggr(mv2[:, t, :], st2[:, t, :])
                    ins.then_inc(s_mv2, 1)
                if on(i, -1):
                    no_sight(i + 1)
                if on(i, -2):
                    normed(i + 2)
            steps(dve, step)

        @block.tensor
        def _(pe):
            def x_T(n):
                pe.wait_ge(s_xh, n + 1)
                wait(pe, s_lgc, n - 2)
                for k in range(KC):
                    for t in range(UT):
                        last = nc.tensor.transpose(p_m[:, (k * UT + t) * P:(k * UT + t + 1) * P],
                                                   xh[:, t, k * P:(k + 1) * P], ident[:, :])
                last.then_inc(s_xT, 1)

            def q_T(n):
                pe.wait_ge(s_xTlo, n + 1)
                for m in range(KC):
                    for k in range(KC):
                        for q, (a, b) in enumerate(PASSES):
                            last = nc.tensor.matmul(p_m[:, m * UT * P:(m + 1) * UT * P], wq[a][:, k, m * P:(m + 1) * P],
                                                    xT[b][:, k, :], start=(k == 0 and q == 0),
                                                    stop=(k == KC - 1 and q == 2))
                last.then_inc(s_q, 1)

            def scores(i, t, m):
                wait(pe, s_exp, 4 * i + 2 * t + m - 1)
                bt = i // UB
                for n in range(2):
                    for q, (a, b) in enumerate(PASSES):
                        c0 = m * HW + n * 4 * SK
                        last = nc.tensor.matmul(p_s[:, 2 * m + n, 0:4 * SK], qT[a][:, m, t * P:(t + 1) * P],
                                                kblk[b][:, bass.ds(bt, 1), c0:c0 + 4 * SK],
                                                start=(q == 0), stop=(q == 2))
                last.then_inc(s_S, 1)

            def prob_T(u, t, gi):
                c0, cn = GROUPS[gi]
                G = 6 * u + 3 * t + gi
                pe.wait_ge(s_P, 4 * u + 2 * t + (1 if gi == 0 else 2))
                wait(pe, s_Tlo, G - 1)
                for c in range(cn):
                    last = nc.tensor.transpose(p_t[(3 * t + gi) % 2][:, c * P:(c + 1) * P],
                                               prob[t][:, (c0 + c) * P:(c0 + c + 1) * P], ident[:, :])
                last.then_inc(s_T, 1)

            def prob_v(u, t, gi):
                c0, cn = GROUPS[gi]
                pe.wait_ge(s_Tlo, 6 * u + 3 * t + gi + 1)
                if gi == 0:
                    wait(pe, s_x1, 2 * u + t)
                bt = u // UB
                for c in range(c0, c0 + cn):
                    rows = HW - 4 * P if c % CH == CH - 1 else P
                    for q, (a, b) in enumerate(PASSES):
                        last = nc.tensor.matmul(p_o[:, 0:H], pT[a][0:rows, c, :],
                                                vp[b][0:rows, bass.ds(bt * (KC * CH) + c, 1), :],
                                                start=(c == 0 and q == 0), stop=(c == KC * CH - 1 and q == 2))
                last.then_inc(s_PV, 1)

            def xn_T(i):
                w = i - 2
                pe.wait_ge(s_qlo, min(i + 1, NU) if isinstance(i, int) else i + 1)
                wait(pe, s_lgc, w)
                pe.wait_ge(s_xn, w + 1)
                for k in range(KC):
                    for t in range(UT):
                        last = nc.tensor.transpose(p_m[:, (k * UT + t) * P:(k * UT + t + 1) * P],
                                                   xn[:, t, k * P:(k + 1) * P], ident[:, :])
                last.then_inc(s_xnT, 1)

            def logits(i):
                pe.wait_ge(s_xnc, i - 1)
                for k in range(KC):
                    last = nc.tensor.matmul(p_m[0:E, 0:UT * P], gwT[:, k, :], xnT[:, k, :],
                                            start=(k == 0), stop=(k == KC - 1))
                last.then_inc(s_lgT, 1)

            def logits_back(i):
                pe.wait_ge(s_lgs, i - 1)
                settle(pe)
                for t in range(UT):
                    last = nc.tensor.transpose(p_m[:, t * E:(t + 1) * E], lgs[:, t * P:(t + 1) * P], ident[0:E, 0:E])
                last.then_inc(s_lg, 1)

            x_T(0)
            q_T(0)

            def step(i):
                for t in range(UT):
                    if on(i, 1):
                        prob_T(i - 1, t, 0)
                        prob_T(i - 1, t, 1)
                    if on(i, 0):
                        if t == 0:
                            pe.wait_ge(s_qlo, i + 1)
                        scores(i, t, 0)
                    if t == 1 and on(i, -1):
                        x_T(i + 1)
                    if t == 0 and on(i, 2):
                        xn_T(i)
                    if on(i, 1):
                        prob_v(i - 1, t, 0)
                        prob_T(i - 1, t, 2)
                    if on(i, 0):
                        scores(i, t, 1)
                    if t == 1 and on(i, -1):
                        q_T(i + 1)
                    if t == 0 and on(i, 2):
                        logits(i)
                    if on(i, 1):
                        prob_v(i - 1, t, 1)
                        prob_v(i - 1, t, 2)
                    if t == 0 and on(i, 2):
                        logits_back(i)
            steps(pe, step)


def route_and_prepare(nc, allocator, v):
    ident, lg, tgf, wgu, wd, slot_of, entry, expert_of, slots = (v[k] for k in (
        "ident", "lg", "tgf", "wgu", "wd", "slot_of", "entry", "expert_of", "slots"))
    st = ExitStack()
    with st:
        sb, ps, sem = allocator(st)
        raw = [sb(f"raw{k}", [P, FC * H]) for k in range(2)]
        zeros = sb("zeros", [P, H])
        below = sb("below", [P, P])
        ones = sb("ones", [P, P])
        one_row = sb("one_row", [P, NT])
        tile_at = sb("tile_at", [1, NS])
        tile_at_i = sb("tile_at_i", [1, NS], i32)
        ex = sb("ex", [P, NT, E])
        pr = sb("pr", [P, NT, E])
        rest = sb("rest", [P, NT, E])
        eq = sb("eq", [P, NT, E])
        pick = [sb(f"pick{k}", [P, NT, E]) for k in range(TOPK)]
        sel = sb("sel", [P, NT, E])
        taken = sb("taken", [P, NT])
        top1 = sb("top1", [P, NT])
        top2 = sb("top2", [P, NT])
        den = sb("den", [P, NT])
        wk = sb("wk", [P, TOPK, NT])
        cum = sb("cum", [P, E, NT])
        total = sb("total", [P, E])
        base = sb("base", [P, E])
        count = sb("count", [P, E])
        padded = sb("padded", [P, E])
        padded_i = sb("padded_i", [P, E], i32)
        start = sb("start", [P, E])
        posf = sb("posf", [P, TOPK, NT])
        ttmp = sb("ttmp", [P, NT, E])
        te = sb("te", [1, NS])
        hit = sb("hit", [1, NS])
        p_w = [ps(f"p_w{k}", [P, 512]) for k in range(4)]
        p_r = ps("p_r", [P, 512])
        s_raw = [sem("s_raw0"), sem("s_raw1")]
        s_tr, s_whi, s_wlo = sem("s_tr"), sem("s_whi"), sem("s_wlo")
        s_z, s_init, s_consts, s_p, s_ex, s_sum, s_tot, s_base, s_route, s_iota = (sem(n) for n in (
            "s_z", "s_init", "s_consts", "s_p", "s_ex", "s_sum", "s_tot", "s_base", "s_route", "s_iota"))
        s_pool = sem("s_pool_chain")
        block = st.enter_context(nc.Block())

        GU = [(k, c0, cn) for k in range(KC) for c0, cn in ((0, 4), (4, 2))]
        DN = [(0, c0, 2) for c0 in range(0, FC, 2)]
        groups = {"g": GU, "u": GU, "d": DN}
        PER = sum(len(groups[m]) for m in "gud")
        BANKS = len(p_w)

        def rows_of(c):
            return min(P, FF - c * P)

        def before(q):
            return sum(len(groups["gud"[i % 3]]) for i in range(q))

        def raw_count(q):
            return sum((16 if i % 3 == 2 else 32) for i in range(q + 1) if i % 2 == q % 2)

        def experts(eng, one):
            one(0, v["sg"], v["su"], v["sd"], E, True)
            for e in range(E):
                one(e + 1, v["eg"][e], v["eu"][e], v["ed"][e], e, False)

        @block.sync
        def _(sp):
            def one(n, g, u, d, slot, first):
                for j, (kind, src) in enumerate((("g", g), ("u", u), ("d", d))):
                    q = 3 * n + j
                    if q >= 2:
                        sp.wait_ge(s_tr, before(q - 1))
                    if kind == "d":
                        sp.dma_start(raw[q % 2][:, 0:KC * FF].rearrange("p (c i) -> p c i", i=FF),
                                     src.rearrange("(c p) i -> p c i", p=P)).then_inc(s_raw[q % 2], 16)
                    else:
                        full = (FC - 1) * P
                        sp.dma_start(raw[q % 2][:, 0:(FC - 1) * H].rearrange("p (c h) -> p c h", h=H),
                                     src[0:full, :].rearrange("(c p) h -> p c h", p=P)).then_inc(s_raw[q % 2], 16)
                        sp.dma_start(raw[q % 2][0:FF - full, (FC - 1) * H:FC * H],
                                     src[full:FF, :]).then_inc(s_raw[q % 2], 16)
            experts(sp, one)
            sp.wait_ge(s_z, 1)
            sp.dma_start(v["xn_d"][N:N + P, :], zeros[:, :]).then_inc(s_init, 16)
            sp.dma_start(v["out"][N:N + P, :], zeros[:, :]).then_inc(s_init, 16)
            sp.wait_ge(s_iota, 1)
            sp.dma_start(v["slots_d"].rearrange("(j p) c -> p j c", p=P), slots[:, :, :]).then_inc(s_init, 16)
            sp.wait_ge(s_init, 48)

        @block.tensor
        def _(pe):
            def one(n, g, u, d, slot, first):
                for j, kind in enumerate("gud"):
                    q = 3 * n + j
                    pe.wait_ge(s_raw[q % 2], raw_count(q))
                    for gi, (k, c0, cn) in enumerate(groups[kind]):
                        G = before(q) + gi
                        if G >= BANKS:
                            pe.wait_ge(s_wlo, G - BANKS + 1)
                        bank = p_w[G % BANKS]
                        for c in range(c0, c0 + cn):
                            r = rows_of(c)
                            if kind == "d":
                                for kk in range(KC):
                                    last = nc.tensor.transpose(bank[0:r, (c - c0) * H + kk * P:(c - c0) * H + (kk + 1) * P],
                                                               raw[q % 2][:, kk * FF + c * P:kk * FF + c * P + r], ident[:, :])
                            else:
                                last = nc.tensor.transpose(bank[:, (c - c0) * P:(c - c0) * P + r],
                                                           raw[q % 2][0:r, c * H + k * P:c * H + (k + 1) * P],
                                                           ident[0:r, 0:r])
                        last.then_inc(s_tr, 1)
                if first:
                    pe.wait_ge(s_tot, 1)
                    pe.wait_ge(s_consts, 2)
                    nc.tensor.matmul(p_r[:, 0:E], below[:, :], total[:, :], start=True, stop=True)
                    nc.tensor.matmul(p_r[:, E:2 * E], ones[:, :], total[:, :], start=True, stop=True).then_inc(s_base, 1)
            experts(pe, one)

        def pieces(kind, k, c0, cn, slot, s, bank):
            if kind == "d":
                if c0 + cn < FC:
                    yield (wd[s][:, slot * FC + c0:slot * FC + c0 + cn, :],
                           bank[:, 0:cn * H].rearrange("p (c h) -> p c h", h=H))
                else:
                    r = rows_of(FC - 1)
                    yield wd[s][:, slot * FC + c0, :], bank[:, 0:H]
                    yield wd[s][0:r, slot * FC + c0 + 1, :], bank[0:r, H:2 * H]
            else:
                o = 0 if kind == "g" else FF
                w = min((c0 + cn) * P, FF) - c0 * P
                yield wgu[s][:, slot * KC + k, o + c0 * P:o + c0 * P + w], bank[:, 0:w]

        @block.scalar
        def _(act):
            def one(n, g, u, d, slot, first):
                if first:
                    act.wait_ge(s_p, 1)
                    act.activation(pr[:, :, :], ex[:, :, :], ACT.Exp).then_inc(s_ex, 1)
                for j, kind in enumerate("gud"):
                    for gi, (k, c0, cn) in enumerate(groups[kind]):
                        G = before(3 * n + j) + gi
                        act.wait_ge(s_tr, G + 1)
                        for dst, src in pieces(kind, k, c0, cn, slot, 0, p_w[G % BANKS]):
                            last = act.activation(dst, src, ACT.Copy)
                        last.then_inc(s_whi, 1)
            experts(act, one)

        @block.gpsimd
        def _(pool):
            pool.memset(zeros[:, :], 0.0).then_inc(s_z, 1)
            pool.memset(below[:, :], 1.0).then_inc(s_pool, 1)
            pool.memset(ones[:, :], 1.0).then_inc(s_consts, 1)
            pool.wait_ge(s_pool, 1)
            pool.affine_select(out=below[:, :], in_=below[:, :], compare_op=ALU.is_gt, fill=0.0, base=0,
                               pattern=[[1, P]], channel_multiplier=-1).then_inc(s_consts, 1)
            pool.iota(slots[:, :, 0], pattern=[[0, NS]], base=N, channel_multiplier=1,
                      allow_small_or_imprecise_dtypes=True).then_inc(s_pool, 1)
            pool.memset(slots[:, :, 1], 0.0).then_inc(s_pool, 1)
            pool.wait_ge(s_pool, 3)
            for k in range(TOPK):
                last = pool.iota(entry[:, k, :, 0], pattern=[[P, NT]], base=0, channel_multiplier=1,
                                 allow_small_or_imprecise_dtypes=True)
            last = pool.iota(tile_at_i[:, :], pattern=[[P, NS]], base=0, channel_multiplier=0)
            last.then_inc(s_iota, 1)

        @block.vector
        def _(dve):
            chain = [0]

            def link(ins):
                chain[0] += 1
                ins.then_inc(s_route, 1)
                dve.wait_ge(s_route, chain[0])

            tt, ts = nc.vector.tensor_tensor, nc.vector.tensor_scalar
            wide = [P, NT, E]

            def first_of(dst, values, top):
                link(tt(eq[:, :, :], values, top[:, :].unsqueeze(2).broadcast_to(wide), ALU.is_equal))
                link(nc.vector.tensor_copy(dst[:, :, 0], eq[:, :, 0]))
                link(nc.vector.tensor_copy(taken[:, :], eq[:, :, 0]))
                for e in range(1, E):
                    link(tt(dst[:, :, e], eq[:, :, e], taken[:, :], ALU.is_gt))
                    link(tt(taken[:, :], taken[:, :], eq[:, :, e], ALU.max))

            def route_1():
                link(nc.vector.tensor_reduce(top1[:, :], lg[:, :, :], AX.X, ALU.max))
                tt(ex[:, :, :], lg[:, :, :], top1[:, :].unsqueeze(2).broadcast_to(wide), ALU.subtract).then_inc(s_p, 1)
                dve.wait_ge(s_ex, 1)
                link(nc.vector.tensor_reduce(den[:, :], pr[:, :, :], AX.X, ALU.add))
                link(nc.vector.reciprocal(den[:, :], den[:, :]))
                link(tt(pr[:, :, :], pr[:, :, :], den[:, :].unsqueeze(2).broadcast_to(wide), ALU.mult))
                link(nc.vector.tensor_reduce(top1[:, :], pr[:, :, :], AX.X, ALU.max))
                first_of(pick[0], pr[:, :, :], top1)
                link(ts(rest[:, :, :], pick[0][:, :, :], -2.0, None, ALU.mult))
                link(tt(rest[:, :, :], rest[:, :, :], pr[:, :, :], ALU.add))
                link(nc.vector.tensor_reduce(top2[:, :], rest[:, :, :], AX.X, ALU.max))
                first_of(pick[1], rest[:, :, :], top2)
                link(tt(sel[:, :, :], pick[0][:, :, :], pick[1][:, :, :], ALU.add))
                link(tt(den[:, :], top1[:, :], top2[:, :], ALU.add))
                link(ts(den[:, :], den[:, :], 1e-20, None, ALU.add))
                link(nc.vector.reciprocal(den[:, :], den[:, :]))
                link(ts(den[:, :], den[:, :], tgf[:, :], None, ALU.mult))
                dve.wait_ge(s_iota, 1)
                link(tt(entry[:, 0, :, 1], top1[:, :], den[:, :], ALU.mult))
                link(tt(entry[:, 1, :, 1], top2[:, :], den[:, :], ALU.mult))
                link(nc.vector.memset(one_row[:, :], 1.0))
                for e in range(E):
                    link(nc.vector.tensor_tensor_scan(cum[:, e, :], one_row[:, :], sel[:, :, e], 0.0,
                                                      ALU.mult, ALU.add))
                nc.vector.tensor_copy(total[:, :], cum[:, :, NT - 1]).then_inc(s_tot, 1)

            def route_2():
                dve.wait_ge(s_base, 1)
                link(nc.vector.tensor_copy(base[:, :], p_r[:, 0:E]))
                link(ts(count[:, :], p_r[:, E:2 * E], float(P - 1), None, ALU.add))
                link(nc.vector.tensor_copy(padded_i[:, :], count[:, :]))
                link(ts(padded_i[:, :], padded_i[:, :], P.bit_length() - 1, P.bit_length() - 1,
                        ALU.arith_shift_right, ALU.logical_shift_left))
                link(nc.vector.tensor_copy(padded[:, :], padded_i[:, :]))
                link(nc.vector.memset(start[:, 0:1], 0.0))
                for e in range(1, E):
                    link(tt(start[:, e:e + 1], start[:, e - 1:e], padded[:, e - 1:e], ALU.add))
                link(tt(base[:, :], base[:, :], start[:, :], ALU.add))
                link(ts(base[:, :], base[:, :], -1.0, None, ALU.add))
                link(tt(cum[:, :, :], cum[:, :, :], base[:, :].unsqueeze(2).broadcast_to([P, E, NT]), ALU.add))
                for k in range(TOPK):
                    link(tt(ttmp[:, :, :], pick[k][:, :, :], cum[:, :, :].rearrange("p e t -> p t e"), ALU.mult))
                    link(nc.vector.tensor_reduce(posf[:, k, :], ttmp[:, :, :], AX.X, ALU.add))
                link(nc.vector.tensor_copy(slot_of[:, :, :], posf[:, :, :]))
                link(nc.vector.tensor_copy(tile_at[:, :], tile_at_i[:, :]))
                link(ts(te[:, :], tile_at[:, :], start[0:1, 1:2], None, ALU.is_ge))
                for e in range(2, E):
                    link(ts(hit[:, :], tile_at[:, :], start[0:1, e:e + 1], None, ALU.is_ge))
                    link(tt(te[:, :], te[:, :], hit[:, :], ALU.add))
                link(nc.vector.tensor_copy(expert_of[:, :], te[:, :]))

            def one(n, g, u, d, slot, first):
                for j, kind in enumerate("gud"):
                    for gi, (k, c0, cn) in enumerate(groups[kind]):
                        G = before(3 * n + j) + gi
                        dve.wait_ge(s_whi, G + 1)
                        for (dst, src), (hi, _) in zip(pieces(kind, k, c0, cn, slot, 1, p_w[G % BANKS]),
                                                       pieces(kind, k, c0, cn, slot, 0, p_w[G % BANKS])):
                            last = tt(dst, src, hi, ALU.subtract)
                        last.then_inc(s_wlo, 1)
                if first:
                    route_2()

            route_1()
            experts(dve, one)


def feed_forward(nc, allocator, v):
    ident, tgf, wgu, wd, slot_of, entry, expert_of, slots = (v[k] for k in (
        "ident", "tgf", "wgu", "wd", "slot_of", "entry", "expert_of", "slots"))
    xn_d, x1_d, out, slots_d = v["xn_d"], v["x1_d"], v["out"], v["slots_d"]
    st = ExitStack()
    with st:
        sb, ps, sem = allocator(st)
        xin = [sb(f"xin{k}", [P, H]) for k in range(2)]
        res = [sb(f"res{k}", [P, H]) for k in range(2)]
        yout = [sb(f"yout{k}", [P, H]) for k in range(2)]
        fxT = [sb(f"fxT_{s}", [P, KC, P], f32r) for s in ("hi", "lo")]
        sil = sb("sil", [P, FF])
        put_in = [sb(f"put_in{k}", [P, PUTS, 2]) for k in range(2)]
        put_at, get_at, add_at = ([sb(f"{n}_at{k}", [P, w], i32) for k in range(2)]
                                  for n, w in (("put", PUTS), ("get", 1), ("add", 1)))
        hid = sb("hid", [P, FC * P])
        hT = [sb(f"hT_{s}", [P, FC, P], f32r) for s in ("hi", "lo")]
        p_gu = ps("p_gu", [P, 4, 512])
        p_x = ps("p_x", [P, 512])
        p_h = ps("p_h", [P, 2, 512])
        p_y = ps("p_y", [P, 512])
        names = ("s_xT s_xhi s_xlo s_gu s_sil s_hid s_hT s_hhi s_hlo s_y s_yo s_pad s_slots "
                 "s_put_at s_get_at s_add_at s_add").split()
        (s_xT, s_xhi, s_xlo, s_gu, s_sil, s_hid, s_hT, s_hhi, s_hlo, s_y, s_yo, s_pad, s_slots,
         s_put_at, s_get_at, s_add_at, s_add) = (sem("f" + n) for n in names)
        s_in = [sem(f"fs_in{k}") for k in range(2)]
        s_res = [sem(f"fs_res{k}") for k in range(2)]
        s_gat = [sem(f"fs_gat{k}") for k in range(2)]
        s_out = [sem(f"fs_out{k}") for k in range(2)]
        s_turn = sem("fs_turn")
        s_put = [sem(f"fs_put{k}") for k in range(2)]
        block = st.enter_context(nc.Block())
        x_t = xn_d[0:N, :].rearrange("(t p) d -> p t d", p=P)
        r_t = x1_d.rearrange("(t p) d -> p t d", p=P)
        o_t = out[0:N, :].rearrange("(t p) d -> p t d", p=P)
        TOTAL = NT + NS

        def tiles(eng, step):
            for j in range(4):
                step(j, j % 2, True)
            with eng.Fori(2, NT // 2 - 1) as h:
                for k in range(2):
                    step(2 * h + k, k, True)
            for j in range(NT - 2, NT + 2):
                step(j, j % 2, j < NT)
            with eng.Fori(NT // 2 + 1, TOTAL // 2 - 1) as h:
                for k in range(2):
                    step(2 * h + k, k, False)
            for j in range(TOTAL - 2, TOTAL):
                step(j, j % 2, False)

        def wait(eng, s, val):
            if isinstance(val, int) and val <= 0:
                return
            eng.wait_ge(s, val)

        def settle(eng):
            eng.sem_inc(s_turn, 1)

        def tile(ap, j):
            return ap[:, bass.ds(j, 1), :].rearrange("p o d -> p (o d)")

        @block.sync
        def _(sp):
            def load(j, k):
                wait(sp, s_xT, j - 1)
                sp.dma_start(xin[k][:, :], tile(x_t, j)).then_inc(s_in[k], 16)
                wait(sp, s_yo, j - 1)
                sp.dma_start(res[k][:, :], tile(r_t, j)).then_inc(s_res[k], 16)
            load(0, 0)
            load(1, 1)
            with sp.Fori(1, NT // 2) as h:
                for k in range(2):
                    load(2 * h + k, k)

        @block.gpsimd
        def _(pool):
            slot_cols = slot_of[:, :, :].rearrange("p k t -> p (k t)")
            entry_cols = entry[:, :, :, :].rearrange("p k t c -> p (k t) c")

            def puts(n, first):
                for r in range(2):
                    if not first:
                        pool.wait_ge(s_put[r], 8 * PUTS * n)
                    pool.tensor_copy(put_at[r][:, :], slot_cols[:, bass.ds((n + r) * PUTS, PUTS)]).then_inc(s_put_at, 1)
                    pool.tensor_copy(put_in[r][:, :, :], entry_cols[:, bass.ds((n + r) * PUTS, PUTS), :]).then_inc(s_put_at, 1)
                    pool.wait_ge(s_put_at, 2 * (n + r + 1))
                    settle(pool)
                    for c in range(PUTS):
                        pool.indirect_dma_start(
                            slots_d, bass.IndirectOffsetOnAxis(put_at[r][:, c:c + 1], 0),
                            put_in[r][:, c, :],
                            None).then_inc(s_put[r], 16)

            puts(0, True)
            with pool.Fori(1, TOPK * NT // PUTS // 2) as n:
                puts(2 * n, False)
            for r in range(2):
                pool.wait_ge(s_put[r], 8 * TOPK * NT)
            pool.dma_start(slots[:, :, :], slots_d.rearrange("(j p) c -> p j c", p=P)).then_inc(s_slots, 16)
            pool.wait_ge(s_slots, 16)

            def gather(j, k):
                wait(pool, s_xT, j - 1)
                pool.tensor_copy(get_at[k][:, :], slots[:, bass.ds(j - NT, 1), 0]).then_inc(s_get_at, 1)
                pool.wait_ge(s_get_at, j - NT + 1)
                settle(pool)
                pool.indirect_dma_start(xin[k][:, :], None, xn_d,
                                        bass.IndirectOffsetOnAxis(get_at[k][:, :], 0)).then_inc(s_gat[k], 16)

            def add(j, k):
                if not (isinstance(j, int) and j < NT + 2):
                    pool.wait_ge(s_add, 16 * (j - NT - 1))
                pool.tensor_copy(add_at[k][:, :], slots[:, bass.ds(j - NT, 1), 0]).then_inc(s_add_at, 1)
                pool.wait_ge(s_add_at, j - NT + 1)
                pool.wait_ge(s_yo, j + 1)
                wait(pool, s_add, 16 * (j - NT))
                settle(pool)
                pool.indirect_dma_start(out, bass.IndirectOffsetOnAxis(add_at[k][:, :], 0),
                                        yout[k][:, :], None, compute_op=ALU.add).then_inc(s_add, 16)

            gather(NT, 0)
            gather(NT + 1, 1)
            gather(NT + 2, 0)
            for k in range(2):
                pool.wait_ge(s_out[k], 16 * (NT // 2))
            for k in range(2):
                gather(NT + k + 3, 1 - k)
                add(NT + k, k)
            with pool.Fori(NT // 2 + 1, TOTAL // 2 - 2) as h:
                for k in range(2):
                    gather(2 * h + k + 3, 1 - k)
                    add(2 * h + k, k)
            for j in range(TOTAL - 4, TOTAL):
                if j + 3 < TOTAL:
                    gather(j + 3, 1 - j % 2)
                add(j, j % 2)
            pool.wait_ge(s_add, 16 * NS)

        @block.scalar
        def _(act):
            def x_hi(j):
                act.wait_ge(s_xT, j + 1)
                wait(act, s_gu, j)
                act.activation(fxT[0][:, :, :], p_x[:, 0:KC * P].rearrange("p (c t) -> p c t", t=P),
                               ACT.Copy).then_inc(s_xhi, 1)

            x_hi(0)

            def step(j, k, shared):
                last = isinstance(j, int) and j == TOTAL - 1
                act.wait_ge(s_gu, j + 1)
                wait(act, s_hid, j)
                act.activation(sil[:, :].rearrange("p (n f) -> p n f", f=FH), p_gu[:, 0:2, 0:FH], ACT.Silu).then_inc(s_sil, 1)
                if not last:
                    x_hi(j + 1)
                if not (isinstance(j, int) and j == 0):
                    send(j - 1, 1 - k, shared if not isinstance(j, int) else j - 1 < NT)
                act.wait_ge(s_hT, j + 1)
                act.activation(hT[0][:, 0:4, :], p_h[:, 0, :].rearrange("p (c t) -> p c t", t=P), ACT.Copy)
                act.activation(hT[0][:, 4:FC, :], p_h[:, 1, 0:2 * P].rearrange("p (c t) -> p c t", t=P),
                               ACT.Copy).then_inc(s_hhi, 1)

            def send(j, k, shared):
                if shared:
                    act.wait_ge(s_yo, j + 1)
                    act.dma_start(tile(o_t, j), yout[k][:, :]).then_inc(s_out[k], 16)
            tiles(act, step)

        @block.vector
        def _(dve):
            nc.vector.memset(hid[:, FF:FC * P], 0.0).then_inc(s_pad, 1)

            def x_lo(j):
                dve.wait_ge(s_xhi, j + 1)
                nc.vector.tensor_tensor(fxT[1][:, :, :], p_x[:, 0:KC * P].rearrange("p (c t) -> p c t", t=P),
                                        fxT[0][:, :, :], ALU.subtract).then_inc(s_xlo, 1)

            def result(j, k, shared):
                dve.wait_ge(s_y, j + 1)
                if shared:
                    half = j // 2
                    wait(dve, s_out[k], 16 * half)
                    dve.wait_ge(s_res[k], 16 * (half + 1))
                    nc.vector.scalar_tensor_tensor(out=yout[k][:, :], in0=p_y[:, 0:H], scalar=tgf[:, :],
                                                   in1=res[k][:, :], op0=ALU.mult, op1=ALU.add).then_inc(s_yo, 1)
                else:
                    if isinstance(j, int) and j < NT + 2:
                        dve.wait_ge(s_out[k], 16 * (NT // 2))
                        dve.wait_ge(s_slots, 16)
                    else:
                        dve.wait_ge(s_add, 16 * (j - NT - 1))
                    nc.vector.tensor_scalar(yout[k][:, :], p_y[:, 0:H], slots[:, bass.ds(j - NT, 1), 1],
                                            None, ALU.mult).then_inc(s_yo, 1)

            x_lo(0)

            def step(j, k, shared):
                last = isinstance(j, int) and j == TOTAL - 1
                dve.wait_ge(s_sil, j + 1)
                wait(dve, s_hT, j)
                nc.vector.tensor_tensor(hid[:, 0:FF].rearrange("p (n f) -> p n f", f=FH), p_gu[:, 2:4, 0:FH],
                                        sil[:, :].rearrange("p (n f) -> p n f", f=FH), ALU.mult).then_inc(s_hid, 1)
                if not last:
                    x_lo(j + 1)
                if not (isinstance(j, int) and j == 0):
                    result(j - 1, 1 - k, shared if not isinstance(j, int) else j - 1 < NT)
                dve.wait_ge(s_hhi, j + 1)
                nc.vector.tensor_tensor(hT[1][:, 0:4, :], p_h[:, 0, :].rearrange("p (c t) -> p c t", t=P),
                                        hT[0][:, 0:4, :], ALU.subtract)
                nc.vector.tensor_tensor(hT[1][:, 4:FC, :], p_h[:, 1, 0:2 * P].rearrange("p (c t) -> p c t", t=P),
                                        hT[0][:, 4:FC, :], ALU.subtract).then_inc(s_hlo, 1)
            tiles(dve, step)
            result(TOTAL - 1, 1, False)

        @block.tensor
        def _(pe):
            def x_T(j, k, shared):
                if shared:
                    pe.wait_ge(s_in[k], 16 * (j // 2 + 1))
                else:
                    pe.wait_ge(s_gat[k], 16 * ((j - NT) // 2 + 1))
                wait(pe, s_xlo, j)
                for c in range(KC):
                    last = nc.tensor.transpose(p_x[:, c * P:(c + 1) * P], xin[k][:, c * P:(c + 1) * P], ident[:, :])
                last.then_inc(s_xT, 1)

            def gate_up(j, e):
                pe.wait_ge(s_xlo, j + 1)
                wait(pe, s_hid, j)
                for c in range(KC):
                    for q, (a, b) in enumerate(PASSES):
                        for n in range(4):
                            last = nc.tensor.matmul(p_gu[:, n, 0:FH], fxT[a][:, c, :],
                                                    wgu[b][:, bass.ds(e * KC + c, 1), n * FH:(n + 1) * FH],
                                                    start=(c == 0 and q == 0), stop=(c == KC - 1 and q == 2))
                last.then_inc(s_gu, 1)

            def down(j, e):
                pe.wait_ge(s_hlo, j + 1)
                wait(pe, s_yo, j)
                for c in range(FC):
                    r = min(P, FF - c * P)
                    for q, (a, b) in enumerate(PASSES):
                        last = nc.tensor.matmul(p_y[:, 0:H], hT[a][0:r, c, :], wd[b][0:r, bass.ds(e * FC + c, 1), :],
                                                start=(c == 0 and q == 0), stop=(c == FC - 1 and q == 2))
                last.then_inc(s_y, 1)

            def hidden_T(j):
                pe.wait_ge(s_hid, j + 1)
                wait(pe, s_hlo, j)
                for c in range(FC):
                    last = nc.tensor.transpose(p_h[:, c // 4, (c % 4) * P:(c % 4 + 1) * P], hid[:, c * P:(c + 1) * P],
                                               ident[:, :])
                last.then_inc(s_hT, 1)

            held = [pe.alloc_register(f"expert_of_tile{k}") for k in range(2)]

            def hold(j, k):
                pe.reg_load(held[k], expert_of[0:1, bass.ds(j - NT, 1)])

            def expert(k):
                return pe.snap(held[k], min_val=0, max_val=E - 1)

            pe.wait_ge(s_pad, 1)
            x_T(0, 0, True)

            def step(j, k, shared):
                fixed = isinstance(j, int)
                gate_up(j, E if shared else expert(k))
                if not (fixed and j == TOTAL - 1):
                    x_T(j + 1, 1 - k, shared if not fixed else j + 1 < NT)
                if not (fixed and j == 0):
                    before_shared = shared if not fixed else j - 1 < NT
                    down(j - 1, E if before_shared else expert(1 - k))
                    next_shared = shared if not fixed else j + 1 < NT
                    if not next_shared and not (fixed and j == TOTAL - 1):
                        hold(j + 1, 1 - k)
                hidden_T(j)
            tiles(pe, step)
            down(TOTAL - 1, expert(1))


_INS = ['x', 'ctx_1024', 'mask_Bx1xSxS2_if1', 'g_xattn', 'g_ffn', 'L0_xattn_w_q', 'L0_xattn_b_q', 'L0_xattn_w_k',
        'L0_xattn_b_k', 'L0_xattn_w_v', 'L0_xattn_b_v', 'L0_xattn_w_o', 'L0_xattn_b_o', 'L0_ffn_gate_w', 'L0_ffn_eg',
        'L0_ffn_eu', 'L0_ffn_ed', 'L0_ffn_sg', 'L0_ffn_su', 'L0_ffn_sd']


def kernel(**inputs):
    import numpy as _np
    import concourse.bacc as _bacc
    from concourse import mybir as _mybir
    from concourse.bass_utils import run_bass_kernel_spmd as _run

    nc = _bacc.Bacc("TRN2", target_bir_lowering=False, num_devices=1)
    arrays, args = {}, []
    for name in _INS:
        a = _np.ascontiguousarray(inputs[name])
        arrays[f"in_{name}"] = a
        args.append(nc.dram_tensor(f"in_{name}", a.shape, _mybir.dt.from_np(a.dtype), kind="ExternalInput").ap())
    args.append(nc.dram_tensor("out_rows", (N + P, H), _mybir.dt.float32, kind="ExternalOutput").ap())
    flamingo(nc, *args)
    r = _run(nc, [arrays], core_ids=[0])
    return r.results[0]["out_rows"][0:N].reshape(B, S, H)
```

```python
import concourse.bass as bass
from concourse import mybir
from contextlib import ExitStack

fp32 = mybir.dt.float32
f32r = mybir.dt.float32r
i32 = mybir.dt.int32
u8 = mybir.dt.uint8
ALU = mybir.AluOpType
ACT = mybir.ActivationFunctionType
AX = mybir.AxisListType

P = 128
B, S, H = 4, 1024, 256
SK = 77
NH, DH = 16, 16
N = B * S
NT = N // P
UT = 2
NU = NT // UT
UB = NU // B
KC = H // P
HH = NH // 2
HW = HH * SK
CH = 5
PW = CH * P
E = 4
EPS = 1e-5
TOPK = 2
PUTS = 8
FF = 688
FC = -(-FF // P)
FH = FF // 2
NS = (N * TOPK + E * (P - 1)) // P
PASSES = ((0, 0), (0, 1), (1, 0))


def flamingo(nc, x, ctx_in, mask, g_x, g_f, w_q, b_q, w_k, b_k, w_v, b_v, w_o, b_o,
             gate_w, eg, eu, ed, sg, su, sd, out):
    xf = x.rearrange("b s h -> (b s) h")
    x1_d = nc.dram_tensor("x1_scratch", (N, H), fp32, kind="Internal").ap()
    xn_d = nc.dram_tensor("xn_scratch", (N + P, H), fp32, kind="Internal").ap()
    slots_d = nc.dram_tensor("slots_scratch", (NS * P, 2), fp32, kind="Internal").ap()
    top = ExitStack()
    with top:
        def allocator(stack):
            def sb(name, shape, dt=fp32):
                return stack.enter_context(nc.sbuf_tensor(name, shape, dt))

            def ps(name, shape, dt=fp32):
                return stack.enter_context(nc.psum_tensor(name, shape, dt))

            def sem(name):
                return stack.enter_context(nc.semaphore(name))
            return sb, ps, sem

        sb, ps, sem = allocator(top)
        ident = sb("ident", [P, P])
        tgx = sb("tgx", [P, 1])
        tgf = sb("tgf", [P, 1])
        lg = sb("lg", [P, NT, E])

        attn = ExitStack()
        with attn:
            asb, aps, asem = allocator(attn)
            kblk = [asb(f"kblk_{s}", [P, B, KC * HW], f32r) for s in ("hi", "lo")]
            vp = [asb(f"vp_{s}", [P, B * KC * CH, H], f32r) for s in ("hi", "lo")]
            wq = [asb(f"wq_{s}", [P, KC, H], f32r) for s in ("hi", "lo")]
            gwT = asb("gwT", [P, KC, E])
            xall = asb("xall", [P, NT, H])
            bq = asb("bq", [P, KC])
            bog = asb("bog", [P, H])
            s_x0 = asem("s_x0")
            s_x = asem("s_x")
            prepare_attention(nc, allocator, locals())
            attention(nc, allocator, locals())

        wgu = [sb(f"wgu_{s}", [P, (E + 1) * KC, 2 * FF], f32r) for s in ("hi", "lo")]
        wd = [sb(f"wd_{s}", [P, (E + 1) * FC, H], f32r) for s in ("hi", "lo")]
        slot_of = sb("slot_of", [P, TOPK, NT], i32)
        entry = sb("entry", [P, TOPK, NT, 2])
        expert_of = sb("expert_of", [1, NS], i32)
        slots = sb("slots", [P, NS, 2])
        route_and_prepare(nc, allocator, locals())
        feed_forward(nc, allocator, locals())


def prepare_attention(nc, allocator, v):
    ident, tgx, tgf, kblk, vp, wq, gwT, xall, bq, bog = (v[k] for k in (
        "ident", "tgx", "tgf", "kblk", "vp", "wq", "gwT", "xall", "bq", "bog"))
    s_x0, s_x = v["s_x0"], v["s_x"]
    st = ExitStack()
    with st:
        sb, ps, sem = allocator(st)
        ctx_sb = sb("ctx_sb", [SK, B, H])
        ctxT = sb("ctxT", [P, KC, B * SK])
        wraw = {n: sb(f"{n}_raw", [P, KC, H]) for n in ("wq", "wk", "wv", "wo")}
        wo = [sb(f"wo_{s}", [P, KC, H], f32r) for s in ("hi", "lo")]
        gw_sb = sb("gw_sb", [E, H])
        bkv = sb("bkv", [P, 2, KC])
        kv = sb("kv", [P, 2, KC, B * SK])
        kv_s = [sb(f"kv_{s}", [P, 2, KC, B * SK], f32r) for s in ("hi", "lo")]
        vblkT = [sb(f"vblkT_{s}", [P, KC, HW], f32r) for s in ("hi", "lo")]
        own = sb("own", [P, HH])
        p_ctx = [ps(f"p_ctx{k}", [P, 512]) for k in range(KC)]
        p_kv = [ps(f"p_kv{k}", [P, 512]) for k in range(2 * KC)]
        p_vp = [ps(f"p_vp{k}", [P, 512]) for k in range(2)]
        s_ctx, s_bkv, s_small, s_gw = sem("s_ctx"), sem("s_bkv"), sem("s_small"), sem("s_gw")
        s_w = {n: sem(f"s_{n}") for n in wraw}
        s_id, s_own = sem("s_id"), sem("s_own")
        s_ctxps, s_ctxT, s_kvps, s_kv, s_kvhi, s_kvlo = (sem(n) for n in (
            "s_ctxps", "s_ctxT", "s_kvps", "s_kv", "s_kvhi", "s_kvlo"))
        s_wqhi, s_wqlo, s_wohi, s_wolo = (sem(n) for n in ("s_wqhi", "s_wqlo", "s_wohi", "s_wolo"))
        s_tg, s_vhi = sem("s_tg"), sem("s_vhi")
        s_vlo, s_vps, s_vphi, s_vplo, s_gwps, s_bog = (sem(n) for n in (
            "s_vlo", "s_vps", "s_vphi", "s_vplo", "s_gwps", "s_bog"))
        block = st.enter_context(nc.Block())

        xt = v["xf"].rearrange("(t p) d -> p t d", p=P)
        VGROUPS = ((0, 2, P), (2, 2, P), (4, 1, HW - 4 * P))

        def vbank(G):
            return (p_vp + p_ctx)[G % 4]

        def block_diagonal(op, dst, j, i, b, m):
            return op(dst.rearrange("p (h k) -> p h k", h=HH),
                      kv_s[i][:, j, m, b * SK:(b + 1) * SK].unsqueeze(1).broadcast_to([P, HH, SK]),
                      own[:, :].unsqueeze(2).broadcast_to([P, HH, SK]), ALU.mult)

        def v_block(eng, op, i, bm, done):
            if bm >= KC:
                eng.wait_ge(s_vps, 3 * (bm - KC + 1))
            block_diagonal(op, vblkT[i][:, bm % KC, :], 1, i, bm // KC, bm % KC).then_inc(done, 1)

        def k_block(op, i, bm):
            b, m = bm // KC, bm % KC
            block_diagonal(op, kblk[i][:, b, m * HW:(m + 1) * HW], 0, i, b, m)

        @block.sync
        def _(sp):
            sp.dma_start(ctx_sb[:, :, :], v["ctx_in"].rearrange("b k d -> k b d")).then_inc(s_ctx, 16)
            for n in ("wv", "wk", "wo", "wq"):
                src = v["w_" + n[1]]
                sp.dma_start(wraw[n][:, :, :], src.rearrange("(c p) d -> p c d", p=P)).then_inc(s_w[n], 16)
                if n == "wv":
                    sp.dma_start(gw_sb[:, :], v["gate_w"]).then_inc(s_gw, 16)
            sp.dma_start(xall[:, 0:UT, :], xt[:, 0:UT, :]).then_inc(s_x0, 16)
            sp.dma_start(xall[:, UT:NT, :], xt[:, UT:NT, :]).then_inc(s_x, 16)

        @block.gpsimd
        def _(pool):
            pool.memset(ident[:, :], 0.0).then_inc(s_id, 1)
            pool.memset(own[:, :], 1.0).then_inc(s_own, 1)
            pool.wait_ge(s_id, 1)
            pool.affine_select(out=ident[:, :], in_=ident[:, :], compare_op=ALU.not_equal, fill=1.0,
                               base=0, pattern=[[-1, P]], channel_multiplier=1).then_inc(s_id, 1)
            pool.wait_ge(s_own, 1)
            pool.affine_select(out=own[:, :], in_=own[:, :], compare_op=ALU.is_ge, fill=0.0,
                               base=0, pattern=[[-DH, HH]], channel_multiplier=1).then_inc(s_own, 1)
            pool.wait_ge(s_own, 2)
            pool.affine_select(out=own[:, :], in_=own[:, :], compare_op=ALU.is_ge, fill=0.0,
                               base=DH - 1, pattern=[[DH, HH]], channel_multiplier=-1).then_inc(s_own, 1)
            pool.wait_ge(s_own, 3)
            pool.wait_ge(s_kvlo, 1)
            v_block(pool, pool.tensor_tensor, 1, 0, s_vlo)
            pool.wait_ge(s_kvlo, 2)
            for bm in range(B * KC):
                if bm + 1 < B * KC:
                    v_block(pool, pool.tensor_tensor, 1, bm + 1, s_vlo)
                k_block(pool.tensor_tensor, 1, bm)

        @block.scalar
        def _(act):
            act.dma_start(bkv[:, 0, :], v["b_k"].rearrange("(c p) -> p c", p=P), allow_slow_non_contiguous=True).then_inc(s_bkv, 16)
            act.dma_start(bkv[:, 1, :], v["b_v"].rearrange("(c p) -> p c", p=P), allow_slow_non_contiguous=True).then_inc(s_bkv, 16)
            act.dma_start(bq[:, :], v["b_q"].rearrange("(c p) -> p c", p=P), allow_slow_non_contiguous=True).then_inc(s_small, 16)
            act.dma_start(bog[:, :], v["b_o"].partition_broadcast(P)).then_inc(s_small, 16)
            act.dma_start(tgx[:, :], v["g_x"].partition_broadcast(P), allow_slow_non_contiguous=True).then_inc(s_small, 16)
            act.dma_start(tgf[:, :], v["g_f"].partition_broadcast(P), allow_slow_non_contiguous=True).then_inc(s_small, 16)
            act.wait_ge(s_w["wo"], 16)
            act.activation(wo[0][:, :, :], wraw["wo"][:, :, :], ACT.Copy).then_inc(s_wohi, 1)
            for n, j in enumerate((1, 0)):
                act.wait_ge(s_kv, 2 * n + 2)
                act.activation(kv_s[0][:, j, :, :], kv[:, j, :, :], ACT.Copy).then_inc(s_kvhi, 1)
            act.wait_ge(s_w["wq"], 16)
            act.activation(wq[0][:, :, :], wraw["wq"][:, :, :], ACT.Copy).then_inc(s_wqhi, 1)
            for bm in range(B * KC):
                for gi, (c0, cn, rows) in enumerate(VGROUPS):
                    G = 3 * bm + gi
                    act.wait_ge(s_vps, G + 1)
                    act.activation(vp[0][0:rows, bm * CH + c0:bm * CH + c0 + cn, :],
                                   vbank(G)[0:rows, 0:cn * H].rearrange("p (c d) -> p c d", d=H),
                                   ACT.Copy).then_inc(s_vphi, 1)
            act.wait_ge(s_small, 64)
            act.activation(tgx[:, :], tgx[:, :], ACT.Tanh).then_inc(s_tg, 1)
            act.activation(tgf[:, :], tgf[:, :], ACT.Tanh).then_inc(s_tg, 1)

        @block.vector
        def _(dve):
            for k in range(KC):
                dve.wait_ge(s_ctxps, k + 1)
                nc.vector.tensor_copy(ctxT[:, k, :], p_ctx[k][:, 0:B * SK]).then_inc(s_ctxT, 1)
            dve.wait_ge(s_gwps, 1)
            nc.vector.tensor_copy(gwT[:, :, :], p_vp[1][:, 0:KC * E].rearrange("p (c e) -> p c e", e=E)).then_inc(s_ctxT, 1)
            dve.wait_ge(s_bkv, 32)
            for n, j in enumerate((1, 0)):
                for m in range(KC):
                    dve.wait_ge(s_kvps, 2 * n + m + 1)
                    nc.vector.tensor_scalar(kv[:, j, m, :], p_kv[2 * j + m][:, 0:B * SK], bkv[:, j, m:m + 1],
                                            DH ** -0.5 if j == 0 else 1.0, ALU.add, ALU.mult).then_inc(s_kv, 1)
            dve.wait_ge(s_wohi, 1)
            nc.vector.tensor_tensor(wo[1][:, :, :], wraw["wo"][:, :, :], wo[0][:, :, :], ALU.subtract).then_inc(s_wolo, 1)
            for n, j in enumerate((1, 0)):
                dve.wait_ge(s_kvhi, n + 1)
                dve.wait_ge(s_kv, 2 * n + 2)
                nc.vector.tensor_tensor(kv_s[1][:, j, :, :], kv[:, j, :, :], kv_s[0][:, j, :, :],
                                        ALU.subtract).then_inc(s_kvlo, 1)
            dve.wait_ge(s_own, 3)
            v_block(dve, nc.vector.tensor_tensor, 0, 0, s_vhi)
            for bm in range(B * KC):
                if bm + 1 < B * KC:
                    v_block(dve, nc.vector.tensor_tensor, 0, bm + 1, s_vhi)
                k_block(nc.vector.tensor_tensor, 0, bm)
                for gi, (c0, cn, rows) in enumerate(VGROUPS):
                    G = 3 * bm + gi
                    dve.wait_ge(s_vphi, G + 1)
                    dst = [vp[i][0:rows, bm * CH + c0:bm * CH + c0 + cn, :] for i in range(2)]
                    nc.vector.tensor_tensor(dst[1], vbank(G)[0:rows, 0:cn * H].rearrange("p (c d) -> p c d", d=H),
                                            dst[0], ALU.subtract).then_inc(s_vplo, 1)
            dve.wait_ge(s_wqhi, 1)
            nc.vector.tensor_tensor(wq[1][:, :, :], wraw["wq"][:, :, :], wq[0][:, :, :], ALU.subtract).then_inc(s_wqlo, 1)
            dve.wait_ge(s_tg, 2)
            dve.wait_ge(s_small, 64)
            nc.vector.tensor_scalar(bog[:, :], bog[:, :], tgx[:, :], None, ALU.mult).then_inc(s_bog, 1)

        @block.tensor
        def _(pe):
            pe.wait_ge(s_id, 2)
            pe.wait_ge(s_ctx, 16)
            for k in range(KC):
                for b in range(B):
                    last = nc.tensor.transpose(p_ctx[k][:, b * SK:(b + 1) * SK], ctx_sb[:, b, k * P:(k + 1) * P],
                                               ident[0:SK, 0:SK])
                last.then_inc(s_ctxps, 1)
            pe.wait_ge(s_gw, 16)
            for k in range(KC):
                last = nc.tensor.transpose(p_vp[1][:, k * E:(k + 1) * E], gw_sb[:, k * P:(k + 1) * P],
                                           ident[0:E, 0:E])
            last.then_inc(s_gwps, 1)
            pe.wait_ge(s_ctxT, KC)
            for j, n in ((1, "wv"), (0, "wk")):
                pe.wait_ge(s_w[n], 16)
                for m in range(KC):
                    for k in range(KC):
                        last = nc.tensor.matmul(p_kv[2 * j + m][:, 0:B * SK], wraw[n][:, k, m * P:(m + 1) * P],
                                                ctxT[:, k, :], start=(k == 0), stop=(k == KC - 1))
                    last.then_inc(s_kvps, 1)
            pe.wait_ge(s_wolo, 1)
            pe.wait_ge(s_ctxT, KC + 1)
            for bm in range(B * KC):
                pe.wait_ge(s_vhi, bm + 1)
                pe.wait_ge(s_vlo, bm + 1)
                for gi, (c0, cn, rows) in enumerate(VGROUPS):
                    G = 3 * bm + gi
                    if G >= 4:
                        pe.wait_ge(s_vplo, G - 3)
                    for c in range(cn):
                        at = (c0 + c) * P
                        for q, (i, j) in enumerate(PASSES):
                            last = nc.tensor.matmul(vbank(G)[0:rows, c * H:(c + 1) * H],
                                                    vblkT[i][:, bm % KC, at:at + rows], wo[j][:, bm % KC, :],
                                                    start=(q == 0), stop=(q == 2))
                    last.then_inc(s_vps, 1)


def attention(nc, allocator, v):
    ident, tgx, kblk, vp, wq, gwT, xall, bq, bog, lg = (v[k] for k in (
        "ident", "tgx", "kblk", "vp", "wq", "gwT", "xall", "bq", "bog", "lg"))
    s_x0, s_x = v["s_x0"], v["s_x"]
    x1_t = v["x1_d"].rearrange("(t p) d -> p t d", p=P)
    xn_t = v["xn_d"][0:N, :].rearrange("(t p) d -> p t d", p=P)
    st = ExitStack()
    with st:
        sb, ps, sem = allocator(st)
        prob = [sb(f"prob{t}", [P, KC * PW]) for t in range(UT)]
        pT = [sb(f"pT_{s}", [P, KC * CH, P], f32r) for s in ("hi", "lo")]
        xh = sb("xh", [P, UT, H])
        xT = [sb(f"xT_{s}", [P, KC, UT * P], f32r) for s in ("hi", "lo")]
        qT = [sb(f"qT_{s}", [P, KC, UT * P], f32r) for s in ("hi", "lo")]
        xn = sb("xn", [P, UT, H])
        xnT = sb("xnT", [P, KC, UT * P])
        st1 = sb("st1", [P, UT, 6])
        mv1 = sb("mv1", [P, UT, 2])
        rs1 = sb("rs1", [P, UT])
        st2 = sb("st2", [P, UT, 6])
        mv2 = sb("mv2", [P, UT, 2])
        rs2 = sb("rs2", [P, UT])
        negmax = sb("negmax", [P, UT, NH])
        rowsum = sb("rowsum", [P, UT, NH])
        rinv = sb("rinv", [P, UT, NH])
        hidden = sb("hidden", [P, 1])
        mask_in = sb("mask_in", [P, UT, SK], i32)
        blind = sb("blind", [P, UT, SK], i32)
        half = sb("half", [P, UT])
        epst = sb("epst", [P, UT])
        p_s = ps("p_s", [P, 2 * KC, 512])
        p_t = [ps(f"p_t{k}", [P, 512]) for k in range(2)]
        p_o = ps("p_o", [P, 512])
        p_m = ps("p_m", [P, 512])
        names = ("s_mask s_blind s_const s_zero s_ln s_mv1 s_ve1 s_rs1 s_xh s_xT s_xThi s_xTlo s_q s_qhi s_qlo s_S s_cp s_max s_exp s_rec s_P "
                 "s_T s_Thi s_Tlo s_PV s_xb s_x1 s_bn2 s_mv2 s_ve2 s_rs2 s_xn s_xnT s_xnc s_lg s_lgc s_st").split()
        g = {n: sem(n) for n in names}
        (s_mask, s_blind, s_const, s_zero, s_ln, s_mv1, s_ve1, s_rs1, s_xh, s_xT, s_xThi, s_xTlo, s_q, s_qhi, s_qlo, s_S, s_cp, s_max, s_exp, s_rec,
         s_P, s_T, s_Thi, s_Tlo, s_PV, s_xb, s_x1, s_bn2, s_mv2, s_ve2, s_rs2, s_xn, s_xnT, s_xnc, s_lg,
         s_lgc, s_st) = (g[n] for n in names)
        block = st.enter_context(nc.Block())
        s_turn = {nc.vector: sem("s_turn_dve"), nc.tensor: sem("s_turn_pe")}
        GROUPS = ((0, 4), (4, 4), (8, 2))
        PASSES = ((0, 0), (0, 1), (1, 0))

        def wait(eng, s, val):
            if isinstance(val, int) and val <= 0:
                return
            eng.wait_ge(s, val)

        def settle(eng):
            eng.sem_inc(s_turn[eng], 1)

        def steps(eng, step):
            for i in range(3):
                step(i)
            with eng.Fori(3, NU - 2) as i:
                step(i)
            for i in range(NU - 2, NU + 2):
                step(i)

        def on(i, lag):
            return not isinstance(i, int) or 0 <= i - lag < NU

        def ahead(i, t):
            if t == 0:
                return (i, 1) if on(i, 1) else None
            return (i + 1, 0) if on(i, 0) else None

        mask_t = v["mask"].rearrange("b o (t p) k -> p (b o t) k", p=P)

        @block.sync
        def _(sp):
            def mask_load(n):
                wait(sp, s_blind, n)
                sp.dma_start(mask_in[:, :, :], mask_t[:, bass.ds(UT * n, UT), :]).then_inc(s_mask, 16)

            mask_load(0)

            def step(i):
                if on(i, -1):
                    mask_load(i + 1)
                if on(i, 2):
                    w = i - 2
                    sp.wait_ge(s_xn, w + 1)
                    sp.dma_start(x1_t[:, bass.ds(2 * w, UT), :], xall[:, bass.ds(2 * w, UT), :]).then_inc(s_st, 16)
                    sp.dma_start(xn_t[:, bass.ds(2 * w, UT), :], xn[:, :, :]).then_inc(s_st, 16)
            steps(sp, step)
            sp.wait_ge(s_st, 32 * NU)

        @block.gpsimd
        def _(pool):
            pool.memset(half[:, :], -0.5).then_inc(s_const, 1)
            pool.memset(epst[:, :], EPS).then_inc(s_const, 1)
            pool.wait_ge(s_const, 2)

            def rstd(mv, rs, s_in, s_mid, s_out, n):
                pool.wait_ge(s_in, n)
                pool.tensor_tensor(rs[:, :], mv[:, :, 1], epst[:, :], ALU.add).then_inc(s_mid, 1)
                pool.wait_ge(s_mid, n)
                pool.tensor_tensor(rs[:, :], rs[:, :], half[:, :], ALU.pow).then_inc(s_out, 1)

            def residual_bias(n):
                pool.wait_ge(s_xh, n + 1)
                pool.tensor_tensor(xall[:, bass.ds(2 * n, UT), :], xall[:, bass.ds(2 * n, UT), :],
                                   bog[:, :].unsqueeze(1).broadcast_to([P, UT, H]), ALU.add).then_inc(s_xb, 1)

            rstd(mv1, rs1, s_mv1, s_ve1, s_rs1, 1)
            residual_bias(0)
            rstd(mv1, rs1, s_mv1, s_ve1, s_rs1, 2)

            def step(i):
                for t in range(UT):
                    for m in range(KC):
                        if t == 1 and m == 1 and on(i, 1):
                            rstd(mv2, rs2, s_mv2, s_ve2, s_rs2, i)
                        if on(i, 0):
                            pool.wait_ge(s_rec, 4 * i + 2 * t + m + 1)
                            pr = prob[t][:, m * PW:m * PW + HW].rearrange("p (h k) -> p h k", k=SK)
                            pool.tensor_tensor(pr, pr, rinv[:, t, m * HH:(m + 1) * HH].unsqueeze(2).broadcast_to(
                                [P, HH, SK]), ALU.mult).then_inc(s_P, 1)
                        if t == 0 and m == 0 and on(i, -1):
                            residual_bias(i + 1)
                        if t == 0 and m == 1 and on(i, -2):
                            rstd(mv1, rs1, s_mv1, s_ve1, s_rs1, i + 3)
            steps(pool, step)

        @block.scalar
        def _(act):
            def xT_hi(n):
                act.wait_ge(s_xT, n + 1)
                act.activation(xT[0][:, :, :], p_m[:, :].rearrange("p (c t) -> p c t", c=KC), ACT.Copy).then_inc(s_xThi, 1)

            def q_hi(n):
                act.wait_ge(s_q, n + 1)
                for m in range(KC):
                    ins = act.activation(qT[0][:, m, :], p_m[:, m * UT * P:(m + 1) * UT * P], ACT.Identity,
                                         bias=bq[:, m:m + 1])
                ins.then_inc(s_qhi, 1)

            def t_hi(i, t, gi):
                c0, cn = GROUPS[gi]
                G = 6 * (i - 1) + 3 * t + gi
                act.wait_ge(s_T, G + 1)
                wait(act, s_PV, G - 2)
                act.activation(pT[0][:, c0:c0 + cn, :],
                               p_t[(3 * t + gi) % 2][:, 0:cn * P].rearrange("p (c t) -> p c t", t=P),
                               ACT.Copy).then_inc(s_Thi, 1)

            def exps(i, t, m):
                act.wait_ge(s_max, 4 * i + 2 * t + m + 1)
                wait(act, s_T, 6 * (i - 1) + 3 * t + 2 + m)
                wait(act, s_P, 4 * (i - 1) + 2 * t + m + 1)
                for h in range(HH):
                    hd = m * HH + h
                    col = (h % 4) * SK
                    ins = act.activation(prob[t][:, m * PW + h * SK:m * PW + (h + 1) * SK],
                                         p_s[:, 2 * m + h // 4, col:col + SK], ACT.Exp,
                                         bias=negmax[:, t, hd:hd + 1],
                                         accum_out=rowsum[:, t, hd:hd + 1])
                ins.then_inc(s_exp, 1)

            xT_hi(0)
            q_hi(0)

            def step(i):
                for t in range(UT):
                    if t == 1 and on(i, -1):
                        xT_hi(i + 1)
                    if t == 0 and on(i, 2):
                        act.wait_ge(s_xnT, i - 1)
                        act.activation(xnT[:, :, :], p_m[:, :].rearrange("p (c t) -> p c t", c=KC),
                                       ACT.Copy).then_inc(s_xnc, 1)
                    if on(i, 0):
                        exps(i, t, 0)
                    if on(i, 1):
                        t_hi(i, t, 2)
                    if t == 1 and on(i, -1):
                        q_hi(i + 1)
                    if ahead(i, t):
                        t_hi(*ahead(i, t), 0)
                    if on(i, 0):
                        exps(i, t, 1)
                    if t == 0 and on(i, 2):
                        act.wait_ge(s_lg, i - 1)
                        act.activation(lg[:, bass.ds(2 * (i - 2), UT), :],
                                       p_m[:, 0:UT * E].rearrange("p (t e) -> p t e", t=UT), ACT.Copy).then_inc(s_lgc, 1)
                    if ahead(i, t):
                        t_hi(*ahead(i, t), 1)
            steps(act, step)

        @block.vector
        def _(dve):
            nc.vector.memset(hidden[:, :], -10000.0)
            for t in range(UT):
                for m in range(KC):
                    ins = nc.vector.memset(prob[t][:, m * PW + HW:(m + 1) * PW], 0.0)
            ins.then_inc(s_zero, 1)
            dve.wait_ge(s_zero, 1)

            def stats(n):
                for t in range(UT):
                    ins = nc.vector.bn_stats(st1[:, t, :], xall[:, bass.ds(2 * n + t, 1), :])
                ins.then_inc(s_ln, 1)
                dve.wait_ge(s_ln, n + 1)
                settle(dve)
                for t in range(UT):
                    ins = nc.vector.bn_aggr(mv1[:, t, :], st1[:, t, :])
                ins.then_inc(s_mv1, 1)

            def normed(n):
                dve.wait_ge(s_rs1, n + 1)
                wait(dve, s_xT, n)
                for t in range(UT):
                    ins = nc.vector.tensor_scalar(xh[:, t, :], xall[:, bass.ds(2 * n + t, 1), :], mv1[:, t, 0:1],
                                                  rs1[:, t:t + 1], ALU.subtract, ALU.mult)
                ins.then_inc(s_xh, 1)

            def xT_lo(n):
                dve.wait_ge(s_xThi, n + 1)
                nc.vector.tensor_tensor(xT[1][:, :, :], p_m[:, :].rearrange("p (c t) -> p c t", c=KC), xT[0][:, :, :],
                                        ALU.subtract).then_inc(s_xTlo, 1)

            def q_lo(n):
                dve.wait_ge(s_qhi, n + 1)
                for m in range(KC):
                    ins = nc.vector.scalar_tensor_tensor(out=qT[1][:, m, :], in0=p_m[:, m * UT * P:(m + 1) * UT * P],
                                                         scalar=bq[:, m:m + 1], in1=qT[0][:, m, :], op0=ALU.add,
                                                         op1=ALU.subtract)
                ins.then_inc(s_qlo, 1)

            def no_sight(n):
                dve.wait_ge(s_mask, 16 * (n + 1))
                nc.vector.tensor_scalar(blind[:, :, :], mask_in[:, :, :], 0.0, None, ALU.is_equal).then_inc(s_blind, 1)

            def half_max(i, t, m):
                dve.wait_ge(s_S, 4 * i + 2 * t + m + 1)
                wait(dve, s_exp, 4 * (i - 1) + 2 * t + m + 1)
                sc = p_s[:, 2 * m:2 * m + 2, 0:4 * SK].rearrange("p n (h k) -> p n h k", k=SK)
                shape = [P, 2, 4, SK]
                dve.wait_ge(s_blind, i + 1)
                settle(dve)
                nc.vector.copy_predicated(
                    sc, blind[:, t, :].unsqueeze(1).unsqueeze(1).broadcast_to(shape),
                    hidden[:, :].unsqueeze(2).unsqueeze(3).broadcast_to(shape)).then_inc(s_cp, 1)
                dve.wait_ge(s_cp, 4 * i + 2 * t + m + 1)
                nc.vector.tensor_reduce(negmax[:, t, m * HH:(m + 1) * HH].rearrange("p (n h) -> p n h", h=4), sc,
                                        AX.X, ALU.max, negate=True).then_inc(s_max, 1)

            def t_lo(i, t, gi):
                c0, cn = GROUPS[gi]
                G = 6 * (i - 1) + 3 * t + gi
                dve.wait_ge(s_Thi, G + 1)
                wait(dve, s_PV, G - 2)
                nc.vector.tensor_tensor(pT[1][:, c0:c0 + cn, :],
                                        p_t[(3 * t + gi) % 2][:, 0:cn * P].rearrange("p (c t) -> p c t", t=P),
                                        pT[0][:, c0:c0 + cn, :], ALU.subtract).then_inc(s_Tlo, 1)

            def recip(i, t, m):
                dve.wait_ge(s_exp, 4 * i + 2 * t + m + 1)
                wait(dve, s_P, 4 * (i - 1) + 2 * t + m + 1)
                nc.vector.reciprocal(rinv[:, t, m * HH:(m + 1) * HH], rowsum[:, t, m * HH:(m + 1) * HH]).then_inc(s_rec, 1)

            dve.wait_ge(s_x0, 16)
            stats(0)
            normed(0)
            no_sight(0)
            xT_lo(0)
            dve.wait_ge(s_x, 16)
            stats(1)
            q_lo(0)

            def step(i):
                for t in range(UT):
                    if t == 0 and on(i, 2):
                        w = i - 2
                        dve.wait_ge(s_rs2, w + 1)
                        wait(dve, s_xnT, w)
                        wait(dve, s_st, 32 * w)
                        for tt in range(UT):
                            ins = nc.vector.tensor_scalar(xn[:, tt, :], xall[:, bass.ds(2 * w + tt, 1), :],
                                                          mv2[:, tt, 0:1], rs2[:, tt:tt + 1],
                                                          ALU.subtract, ALU.mult)
                        ins.then_inc(s_xn, 1)
                    if on(i, 0):
                        half_max(i, t, 0)
                    if t == 0 and on(i, -1):
                        normed(i + 1)
                    if t == 0 and on(i, -2):
                        stats(i + 2)
                    if t == 1 and on(i, -1):
                        xT_lo(i + 1)
                    if on(i, 0):
                        half_max(i, t, 1)
                        recip(i, t, 0)
                    if on(i, 1):
                        t_lo(i, t, 2)
                    if t == 1 and on(i, -1):
                        q_lo(i + 1)
                    if ahead(i, t):
                        t_lo(*ahead(i, t), 0)
                    if on(i, 1):
                        u = i - 1
                        dve.wait_ge(s_PV, 6 * u + 3 * t + 3)
                        wait(dve, s_xb, u + 1)
                        nc.vector.scalar_tensor_tensor(
                            out=xall[:, bass.ds(2 * u + t, 1), :], in0=p_o[:, 0:H], scalar=tgx[:, :],
                            in1=xall[:, bass.ds(2 * u + t, 1), :], op0=ALU.mult, op1=ALU.add).then_inc(s_x1, 1)
                        dve.wait_ge(s_x1, 2 * u + t + 1)
                        settle(dve)
                        nc.vector.bn_stats(st2[:, t, :], xall[:, bass.ds(2 * u + t, 1), :]).then_inc(s_bn2, 1)
                    if t == 1 and on(i, 1):
                        dve.wait_ge(s_bn2, 2 * i)
                        settle(dve)
                        for tt in range(UT):
                            ins = nc.vector.bn_aggr(mv2[:, tt, :], st2[:, tt, :])
                        ins.then_inc(s_mv2, 1)
                    if on(i, 0):
                        recip(i, t, 1)
                    if ahead(i, t):
                        t_lo(*ahead(i, t), 1)
                if on(i, -1):
                    no_sight(i + 1)
            steps(dve, step)

        @block.tensor
        def _(pe):
            def x_T(n):
                pe.wait_ge(s_xh, n + 1)
                wait(pe, s_lgc, n - 2)
                for k in range(KC):
                    for t in range(UT):
                        last = nc.tensor.transpose(p_m[:, (k * UT + t) * P:(k * UT + t + 1) * P],
                                                   xh[:, t, k * P:(k + 1) * P], ident[:, :])
                last.then_inc(s_xT, 1)

            def q_T(n):
                pe.wait_ge(s_xTlo, n + 1)
                for m in range(KC):
                    for k in range(KC):
                        for q, (a, b) in enumerate(PASSES):
                            last = nc.tensor.matmul(p_m[:, m * UT * P:(m + 1) * UT * P], wq[a][:, k, m * P:(m + 1) * P],
                                                    xT[b][:, k, :], start=(k == 0 and q == 0),
                                                    stop=(k == KC - 1 and q == 2))
                last.then_inc(s_q, 1)

            def scores(i, t, m):
                wait(pe, s_exp, 4 * i + 2 * t + m - 1)
                bt = i // UB
                for n in range(2):
                    for q, (a, b) in enumerate(PASSES):
                        c0 = m * HW + n * 4 * SK
                        last = nc.tensor.matmul(p_s[:, 2 * m + n, 0:4 * SK], qT[a][:, m, t * P:(t + 1) * P],
                                                kblk[b][:, bass.ds(bt, 1), c0:c0 + 4 * SK],
                                                start=(q == 0), stop=(q == 2))
                last.then_inc(s_S, 1)

            def prob_T(u, t, gi):
                c0, cn = GROUPS[gi]
                G = 6 * u + 3 * t + gi
                pe.wait_ge(s_P, 4 * u + 2 * t + (1 if gi == 0 else 2))
                wait(pe, s_Tlo, G - 1)
                for c in range(cn):
                    last = nc.tensor.transpose(p_t[(3 * t + gi) % 2][:, c * P:(c + 1) * P],
                                               prob[t][:, (c0 + c) * P:(c0 + c + 1) * P], ident[:, :])
                last.then_inc(s_T, 1)

            def prob_v(u, t, gi):
                c0, cn = GROUPS[gi]
                pe.wait_ge(s_Tlo, 6 * u + 3 * t + gi + 1)
                if gi == 0:
                    wait(pe, s_x1, 2 * u + t)
                bt = u // UB
                for c in range(c0, c0 + cn):
                    rows = HW - 4 * P if c % CH == CH - 1 else P
                    for q, (a, b) in enumerate(PASSES):
                        last = nc.tensor.matmul(p_o[:, 0:H], pT[a][0:rows, c, :],
                                                vp[b][0:rows, bass.ds(bt * (KC * CH) + c, 1), :],
                                                start=(c == 0 and q == 0), stop=(c == KC * CH - 1 and q == 2))
                last.then_inc(s_PV, 1)

            def xn_T(i):
                w = i - 2
                pe.wait_ge(s_qlo, min(i + 1, NU) if isinstance(i, int) else i + 1)
                pe.wait_ge(s_xn, w + 1)
                for k in range(KC):
                    for t in range(UT):
                        last = nc.tensor.transpose(p_m[:, (k * UT + t) * P:(k * UT + t + 1) * P],
                                                   xn[:, t, k * P:(k + 1) * P], ident[:, :])
                last.then_inc(s_xnT, 1)

            def logits(i):
                pe.wait_ge(s_xnc, i - 1)
                for t in range(UT):
                    for k in range(KC):
                        last = nc.tensor.matmul(p_m[:, t * E:(t + 1) * E], xnT[:, k, t * P:(t + 1) * P],
                                                gwT[:, k, :], start=(k == 0), stop=(k == KC - 1))
                last.then_inc(s_lg, 1)

            x_T(0)
            q_T(0)

            def step(i):
                for t in range(UT):
                    if on(i, 0):
                        if t == 0:
                            pe.wait_ge(s_qlo, i + 1)
                        scores(i, t, 0)
                    if t == 1 and on(i, -1):
                        x_T(i + 1)
                    if on(i, 1):
                        prob_v(i - 1, t, 0)
                    if on(i, 1):
                        prob_T(i - 1, t, 2)
                    if on(i, 0):
                        scores(i, t, 1)
                    if t == 1 and on(i, -1):
                        q_T(i + 1)
                    if t == 0 and on(i, 2):
                        xn_T(i)
                    nxt = ahead(i, t)
                    if nxt:
                        prob_T(nxt[0] - 1, nxt[1], 0)
                    if on(i, 1):
                        prob_v(i - 1, t, 1)
                    if t == 0 and on(i, 2):
                        logits(i)
                    if nxt:
                        prob_T(nxt[0] - 1, nxt[1], 1)
                    if on(i, 1):
                        prob_v(i - 1, t, 2)
            steps(pe, step)


def route_and_prepare(nc, allocator, v):
    ident, lg, tgf, wgu, wd, slot_of, entry, expert_of, slots = (v[k] for k in (
        "ident", "lg", "tgf", "wgu", "wd", "slot_of", "entry", "expert_of", "slots"))
    st = ExitStack()
    with st:
        sb, ps, sem = allocator(st)
        raw = [sb(f"raw{k}", [P, FC * H]) for k in range(2)]
        zeros = sb("zeros", [P, H])
        below = sb("below", [P, P])
        ones = sb("ones", [P, P])
        one_row = sb("one_row", [P, NT])
        tile_at = sb("tile_at", [1, NS])
        tile_at_i = sb("tile_at_i", [1, NS], i32)
        ex = sb("ex", [P, NT, E])
        pr = sb("pr", [P, NT, E])
        rest = sb("rest", [P, NT, E])
        eq = sb("eq", [P, NT, E])
        pick = [sb(f"pick{k}", [P, NT, E]) for k in range(TOPK)]
        sel = sb("sel", [P, NT, E])
        taken = sb("taken", [P, NT])
        top1 = sb("top1", [P, NT])
        top2 = sb("top2", [P, NT])
        den = sb("den", [P, NT])
        wk = sb("wk", [P, TOPK, NT])
        cum = sb("cum", [P, E, NT])
        total = sb("total", [P, E])
        base = sb("base", [P, E])
        count = sb("count", [P, E])
        padded = sb("padded", [P, E])
        padded_i = sb("padded_i", [P, E], i32)
        start = sb("start", [P, E])
        posf = sb("posf", [P, TOPK, NT])
        ttmp = sb("ttmp", [P, NT, E])
        te = sb("te", [1, NS])
        hit = sb("hit", [1, NS])
        p_w = [ps(f"p_w{k}", [P, 512]) for k in range(4)]
        p_r = ps("p_r", [P, 512])
        s_raw = [sem("s_raw0"), sem("s_raw1")]
        s_tr, s_whi, s_wlo = sem("s_tr"), sem("s_whi"), sem("s_wlo")
        s_z, s_init, s_consts, s_p, s_ex, s_sum, s_tot, s_base, s_route, s_iota = (sem(n) for n in (
            "s_z", "s_init", "s_consts", "s_p", "s_ex", "s_sum", "s_tot", "s_base", "s_route", "s_iota"))
        s_pool = sem("s_pool_chain")
        block = st.enter_context(nc.Block())

        GU = [(k, c0, cn) for k in range(KC) for c0, cn in ((0, 4), (4, 2))]
        DN = [(0, c0, 2) for c0 in range(0, FC, 2)]
        groups = {"g": GU, "u": GU, "d": DN}
        PER = sum(len(groups[m]) for m in "gud")
        BANKS = len(p_w)

        def rows_of(c):
            return min(P, FF - c * P)

        def before(q):
            return sum(len(groups["gud"[i % 3]]) for i in range(q))

        def raw_count(q):
            return sum((16 if i % 3 == 2 else 32) for i in range(q + 1) if i % 2 == q % 2)

        def experts(eng, one):
            one(0, v["sg"], v["su"], v["sd"], E, True)
            for e in range(E):
                one(e + 1, v["eg"][e], v["eu"][e], v["ed"][e], e, False)

        @block.sync
        def _(sp):
            def one(n, g, u, d, slot, first):
                for j, (kind, src) in enumerate((("g", g), ("u", u), ("d", d))):
                    q = 3 * n + j
                    if q >= 2:
                        sp.wait_ge(s_tr, before(q - 1))
                    if kind == "d":
                        sp.dma_start(raw[q % 2][:, 0:KC * FF].rearrange("p (c i) -> p c i", i=FF),
                                     src.rearrange("(c p) i -> p c i", p=P)).then_inc(s_raw[q % 2], 16)
                    else:
                        full = (FC - 1) * P
                        sp.dma_start(raw[q % 2][:, 0:(FC - 1) * H].rearrange("p (c h) -> p c h", h=H),
                                     src[0:full, :].rearrange("(c p) h -> p c h", p=P)).then_inc(s_raw[q % 2], 16)
                        sp.dma_start(raw[q % 2][0:FF - full, (FC - 1) * H:FC * H],
                                     src[full:FF, :]).then_inc(s_raw[q % 2], 16)
            experts(sp, one)
            sp.wait_ge(s_z, 1)
            sp.dma_start(v["xn_d"][N:N + P, :], zeros[:, :]).then_inc(s_init, 16)
            sp.dma_start(v["out"][N:N + P, :], zeros[:, :]).then_inc(s_init, 16)
            sp.wait_ge(s_iota, 1)
            sp.dma_start(v["slots_d"].rearrange("(j p) c -> p j c", p=P), slots[:, :, :]).then_inc(s_init, 16)
            sp.wait_ge(s_init, 48)

        @block.tensor
        def _(pe):
            def one(n, g, u, d, slot, first):
                for j, kind in enumerate("gud"):
                    q = 3 * n + j
                    pe.wait_ge(s_raw[q % 2], raw_count(q))
                    for gi, (k, c0, cn) in enumerate(groups[kind]):
                        G = before(q) + gi
                        if G >= BANKS:
                            pe.wait_ge(s_wlo, G - BANKS + 1)
                        bank = p_w[G % BANKS]
                        for c in range(c0, c0 + cn):
                            r = rows_of(c)
                            if kind == "d":
                                for kk in range(KC):
                                    last = nc.tensor.transpose(bank[0:r, (c - c0) * H + kk * P:(c - c0) * H + (kk + 1) * P],
                                                               raw[q % 2][:, kk * FF + c * P:kk * FF + c * P + r], ident[:, :])
                            else:
                                last = nc.tensor.transpose(bank[:, (c - c0) * P:(c - c0) * P + r],
                                                           raw[q % 2][0:r, c * H + k * P:c * H + (k + 1) * P],
                                                           ident[0:r, 0:r])
                        last.then_inc(s_tr, 1)
                if first:
                    pe.wait_ge(s_tot, 1)
                    pe.wait_ge(s_consts, 2)
                    nc.tensor.matmul(p_r[:, 0:E], below[:, :], total[:, :], start=True, stop=True)
                    nc.tensor.matmul(p_r[:, E:2 * E], ones[:, :], total[:, :], start=True, stop=True).then_inc(s_base, 1)
            experts(pe, one)

        def pieces(kind, k, c0, cn, slot, s, bank):
            if kind == "d":
                if c0 + cn < FC:
                    yield (wd[s][:, slot * FC + c0:slot * FC + c0 + cn, :],
                           bank[:, 0:cn * H].rearrange("p (c h) -> p c h", h=H))
                else:
                    r = rows_of(FC - 1)
                    yield wd[s][:, slot * FC + c0, :], bank[:, 0:H]
                    yield wd[s][0:r, slot * FC + c0 + 1, :], bank[0:r, H:2 * H]
            else:
                o = 0 if kind == "g" else FF
                w = min((c0 + cn) * P, FF) - c0 * P
                yield wgu[s][:, slot * KC + k, o + c0 * P:o + c0 * P + w], bank[:, 0:w]

        @block.scalar
        def _(act):
            def one(n, g, u, d, slot, first):
                if first:
                    act.wait_ge(s_p, 1)
                    act.activation(pr[:, :, :], ex[:, :, :], ACT.Exp).then_inc(s_ex, 1)
                for j, kind in enumerate("gud"):
                    for gi, (k, c0, cn) in enumerate(groups[kind]):
                        G = before(3 * n + j) + gi
                        act.wait_ge(s_tr, G + 1)
                        for dst, src in pieces(kind, k, c0, cn, slot, 0, p_w[G % BANKS]):
                            last = act.activation(dst, src, ACT.Copy)
                        last.then_inc(s_whi, 1)
            experts(act, one)

        @block.gpsimd
        def _(pool):
            pool.memset(zeros[:, :], 0.0).then_inc(s_z, 1)
            pool.memset(below[:, :], 1.0).then_inc(s_pool, 1)
            pool.memset(ones[:, :], 1.0).then_inc(s_consts, 1)
            pool.wait_ge(s_pool, 1)
            pool.affine_select(out=below[:, :], in_=below[:, :], compare_op=ALU.is_gt, fill=0.0, base=0,
                               pattern=[[1, P]], channel_multiplier=-1).then_inc(s_consts, 1)
            pool.iota(slots[:, :, 0], pattern=[[0, NS]], base=N, channel_multiplier=1,
                      allow_small_or_imprecise_dtypes=True).then_inc(s_pool, 1)
            pool.memset(slots[:, :, 1], 0.0).then_inc(s_pool, 1)
            pool.wait_ge(s_pool, 3)
            for k in range(TOPK):
                last = pool.iota(entry[:, k, :, 0], pattern=[[P, NT]], base=0, channel_multiplier=1,
                                 allow_small_or_imprecise_dtypes=True)
            last = pool.iota(tile_at_i[:, :], pattern=[[P, NS]], base=0, channel_multiplier=0)
            last.then_inc(s_iota, 1)

        @block.vector
        def _(dve):
            chain = [0]

            def link(ins):
                chain[0] += 1
                ins.then_inc(s_route, 1)
                dve.wait_ge(s_route, chain[0])

            tt, ts = nc.vector.tensor_tensor, nc.vector.tensor_scalar
            wide = [P, NT, E]

            def first_of(dst, values, top):
                link(tt(eq[:, :, :], values, top[:, :].unsqueeze(2).broadcast_to(wide), ALU.is_equal))
                link(nc.vector.tensor_copy(dst[:, :, 0], eq[:, :, 0]))
                link(nc.vector.tensor_copy(taken[:, :], eq[:, :, 0]))
                for e in range(1, E):
                    link(tt(dst[:, :, e], eq[:, :, e], taken[:, :], ALU.is_gt))
                    link(tt(taken[:, :], taken[:, :], eq[:, :, e], ALU.max))

            def route_1():
                link(nc.vector.tensor_reduce(top1[:, :], lg[:, :, :], AX.X, ALU.max))
                tt(ex[:, :, :], lg[:, :, :], top1[:, :].unsqueeze(2).broadcast_to(wide), ALU.subtract).then_inc(s_p, 1)
                dve.wait_ge(s_ex, 1)
                link(nc.vector.tensor_reduce(den[:, :], pr[:, :, :], AX.X, ALU.add))
                link(nc.vector.reciprocal(den[:, :], den[:, :]))
                link(tt(pr[:, :, :], pr[:, :, :], den[:, :].unsqueeze(2).broadcast_to(wide), ALU.mult))
                link(nc.vector.tensor_reduce(top1[:, :], pr[:, :, :], AX.X, ALU.max))
                first_of(pick[0], pr[:, :, :], top1)
                link(ts(rest[:, :, :], pick[0][:, :, :], -2.0, None, ALU.mult))
                link(tt(rest[:, :, :], rest[:, :, :], pr[:, :, :], ALU.add))
                link(nc.vector.tensor_reduce(top2[:, :], rest[:, :, :], AX.X, ALU.max))
                first_of(pick[1], rest[:, :, :], top2)
                link(tt(sel[:, :, :], pick[0][:, :, :], pick[1][:, :, :], ALU.add))
                link(tt(den[:, :], top1[:, :], top2[:, :], ALU.add))
                link(ts(den[:, :], den[:, :], 1e-20, None, ALU.add))
                link(nc.vector.reciprocal(den[:, :], den[:, :]))
                link(ts(den[:, :], den[:, :], tgf[:, :], None, ALU.mult))
                dve.wait_ge(s_iota, 1)
                link(tt(entry[:, 0, :, 1], top1[:, :], den[:, :], ALU.mult))
                link(tt(entry[:, 1, :, 1], top2[:, :], den[:, :], ALU.mult))
                link(nc.vector.memset(one_row[:, :], 1.0))
                for e in range(E):
                    link(nc.vector.tensor_tensor_scan(cum[:, e, :], one_row[:, :], sel[:, :, e], 0.0,
                                                      ALU.mult, ALU.add))
                nc.vector.tensor_copy(total[:, :], cum[:, :, NT - 1]).then_inc(s_tot, 1)

            def route_2():
                dve.wait_ge(s_base, 1)
                link(nc.vector.tensor_copy(base[:, :], p_r[:, 0:E]))
                link(ts(count[:, :], p_r[:, E:2 * E], float(P - 1), None, ALU.add))
                link(nc.vector.tensor_copy(padded_i[:, :], count[:, :]))
                link(ts(padded_i[:, :], padded_i[:, :], P.bit_length() - 1, P.bit_length() - 1,
                        ALU.arith_shift_right, ALU.logical_shift_left))
                link(nc.vector.tensor_copy(padded[:, :], padded_i[:, :]))
                link(nc.vector.memset(start[:, 0:1], 0.0))
                for e in range(1, E):
                    link(tt(start[:, e:e + 1], start[:, e - 1:e], padded[:, e - 1:e], ALU.add))
                link(tt(base[:, :], base[:, :], start[:, :], ALU.add))
                link(ts(base[:, :], base[:, :], -1.0, None, ALU.add))
                link(tt(cum[:, :, :], cum[:, :, :], base[:, :].unsqueeze(2).broadcast_to([P, E, NT]), ALU.add))
                for k in range(TOPK):
                    link(tt(ttmp[:, :, :], pick[k][:, :, :], cum[:, :, :].rearrange("p e t -> p t e"), ALU.mult))
                    link(nc.vector.tensor_reduce(posf[:, k, :], ttmp[:, :, :], AX.X, ALU.add))
                link(nc.vector.tensor_copy(slot_of[:, :, :], posf[:, :, :]))
                link(nc.vector.tensor_copy(tile_at[:, :], tile_at_i[:, :]))
                link(ts(te[:, :], tile_at[:, :], start[0:1, 1:2], None, ALU.is_ge))
                for e in range(2, E):
                    link(ts(hit[:, :], tile_at[:, :], start[0:1, e:e + 1], None, ALU.is_ge))
                    link(tt(te[:, :], te[:, :], hit[:, :], ALU.add))
                link(nc.vector.tensor_copy(expert_of[:, :], te[:, :]))

            def one(n, g, u, d, slot, first):
                for j, kind in enumerate("gud"):
                    for gi, (k, c0, cn) in enumerate(groups[kind]):
                        G = before(3 * n + j) + gi
                        dve.wait_ge(s_whi, G + 1)
                        for (dst, src), (hi, _) in zip(pieces(kind, k, c0, cn, slot, 1, p_w[G % BANKS]),
                                                       pieces(kind, k, c0, cn, slot, 0, p_w[G % BANKS])):
                            last = tt(dst, src, hi, ALU.subtract)
                        last.then_inc(s_wlo, 1)
                if first:
                    route_2()

            route_1()
            experts(dve, one)


def feed_forward(nc, allocator, v):
    ident, tgf, wgu, wd, slot_of, entry, expert_of, slots = (v[k] for k in (
        "ident", "tgf", "wgu", "wd", "slot_of", "entry", "expert_of", "slots"))
    xn_d, x1_d, out, slots_d = v["xn_d"], v["x1_d"], v["out"], v["slots_d"]
    st = ExitStack()
    with st:
        sb, ps, sem = allocator(st)
        xin = [sb(f"xin{k}", [P, H]) for k in range(2)]
        res = [sb(f"res{k}", [P, H]) for k in range(2)]
        yout = [sb(f"yout{k}", [P, H]) for k in range(2)]
        fxT = [sb(f"fxT_{s}", [P, KC, P], f32r) for s in ("hi", "lo")]
        sil = sb("sil", [P, FF])
        put_in = [sb(f"put_in{k}", [P, PUTS, 2]) for k in range(2)]
        put_at, get_at, add_at = ([sb(f"{n}_at{k}", [P, w], i32) for k in range(2)]
                                  for n, w in (("put", PUTS), ("get", 1), ("add", 1)))
        hid = sb("hid", [P, FC * P])
        hT = [sb(f"hT_{s}", [P, FC, P], f32r) for s in ("hi", "lo")]
        p_gu = ps("p_gu", [P, 4, 512])
        p_x = ps("p_x", [P, 512])
        p_h = ps("p_h", [P, 2, 512])
        p_y = ps("p_y", [P, 512])
        names = ("s_xT s_xhi s_xlo s_gu s_sil s_hid s_hT s_hhi s_hlo s_y s_yo s_pad s_slots "
                 "s_put_at s_get_at s_add_at s_add").split()
        (s_xT, s_xhi, s_xlo, s_gu, s_sil, s_hid, s_hT, s_hhi, s_hlo, s_y, s_yo, s_pad, s_slots,
         s_put_at, s_get_at, s_add_at, s_add) = (sem("f" + n) for n in names)
        s_in = [sem(f"fs_in{k}") for k in range(2)]
        s_res = [sem(f"fs_res{k}") for k in range(2)]
        s_gat = [sem(f"fs_gat{k}") for k in range(2)]
        s_out = [sem(f"fs_out{k}") for k in range(2)]
        s_turn = sem("fs_turn")
        s_put = [sem(f"fs_put{k}") for k in range(2)]
        block = st.enter_context(nc.Block())
        x_t = xn_d[0:N, :].rearrange("(t p) d -> p t d", p=P)
        r_t = x1_d.rearrange("(t p) d -> p t d", p=P)
        o_t = out[0:N, :].rearrange("(t p) d -> p t d", p=P)
        TOTAL = NT + NS

        def tiles(eng, step):
            for j in range(4):
                step(j, j % 2, True)
            with eng.Fori(2, NT // 2 - 1) as h:
                for k in range(2):
                    step(2 * h + k, k, True)
            for j in range(NT - 2, NT + 2):
                step(j, j % 2, j < NT)
            with eng.Fori(NT // 2 + 1, (TOTAL - 1) // 2) as h:
                for k in range(2):
                    step(2 * h + k, k, False)
            for j in range((TOTAL - 1) // 2 * 2, TOTAL):
                step(j, j % 2, False)

        def wait(eng, s, val):
            if isinstance(val, int) and val <= 0:
                return
            eng.wait_ge(s, val)

        def settle(eng):
            eng.sem_inc(s_turn, 1)

        def tile(ap, j):
            return ap[:, bass.ds(j, 1), :].rearrange("p o d -> p (o d)")

        @block.sync
        def _(sp):
            def load_x(j, k):
                wait(sp, s_xT, j - 1)
                sp.dma_start(xin[k][:, :], tile(x_t, j)).then_inc(s_in[k], 16)

            def load_res(j, k):
                wait(sp, s_yo, j - 1)
                sp.dma_start(res[k][:, :], tile(r_t, j)).then_inc(s_res[k], 16)

            load_x(0, 0)
            load_x(1, 1)
            load_res(0, 0)
            load_x(2, 0)
            load_res(1, 1)
            with sp.Fori(1, NT // 2 - 1) as h:
                for k in range(2):
                    load_x(2 * h + k + 1, 1 - k)
                    load_res(2 * h + k, k)
            load_x(NT - 1, 1)
            load_res(NT - 2, 0)
            load_res(NT - 1, 1)

        @block.gpsimd
        def _(pool):
            slot_cols = slot_of[:, :, :].rearrange("p k t -> p (k t)")
            entry_cols = entry[:, :, :, :].rearrange("p k t c -> p (k t) c")

            def puts(n, first):
                for r in range(2):
                    if not first:
                        pool.wait_ge(s_put[r], 8 * PUTS * n)
                    pool.tensor_copy(put_at[r][:, :], slot_cols[:, bass.ds((n + r) * PUTS, PUTS)]).then_inc(s_put_at, 1)
                    pool.tensor_copy(put_in[r][:, :, :], entry_cols[:, bass.ds((n + r) * PUTS, PUTS), :]).then_inc(s_put_at, 1)
                    pool.wait_ge(s_put_at, 2 * (n + r + 1))
                    settle(pool)
                    for c in range(PUTS):
                        pool.indirect_dma_start(
                            slots_d, bass.IndirectOffsetOnAxis(put_at[r][:, c:c + 1], 0),
                            put_in[r][:, c, :],
                            None).then_inc(s_put[r], 16)

            puts(0, True)
            with pool.Fori(1, TOPK * NT // PUTS // 2) as n:
                puts(2 * n, False)
            for r in range(2):
                pool.wait_ge(s_put[r], 8 * TOPK * NT)
            pool.dma_start(slots[:, :, :], slots_d.rearrange("(j p) c -> p j c", p=P)).then_inc(s_slots, 16)
            pool.wait_ge(s_slots, 16)

            def gather(j, k):
                wait(pool, s_xT, j - 1)
                pool.tensor_copy(get_at[k][:, :], slots[:, bass.ds(j - NT, 1), 0]).then_inc(s_get_at, 1)
                pool.wait_ge(s_get_at, j - NT + 1)
                settle(pool)
                pool.indirect_dma_start(xin[k][:, :], None, xn_d,
                                        bass.IndirectOffsetOnAxis(get_at[k][:, :], 0)).then_inc(s_gat[k], 16)

            def add(j, k):
                if not (isinstance(j, int) and j < NT + 2):
                    pool.wait_ge(s_add, 16 * (j - NT - 1))
                pool.tensor_copy(add_at[k][:, :], slots[:, bass.ds(j - NT, 1), 0]).then_inc(s_add_at, 1)
                pool.wait_ge(s_add_at, j - NT + 1)
                pool.wait_ge(s_yo, j + 1)
                wait(pool, s_add, 16 * (j - NT))
                settle(pool)
                pool.indirect_dma_start(out, bass.IndirectOffsetOnAxis(add_at[k][:, :], 0),
                                        yout[k][:, :], None, compute_op=ALU.add).then_inc(s_add, 16)

            gather(NT, 0)
            gather(NT + 1, 1)
            gather(NT + 2, 0)
            for k in range(2):
                pool.wait_ge(s_out[k], 16 * (NT // 2))
            for k in range(2):
                gather(NT + k + 3, 1 - k)
                add(NT + k, k)
            with pool.Fori(NT // 2 + 1, (TOTAL - 3) // 2) as h:
                for k in range(2):
                    gather(2 * h + k + 3, 1 - k)
                    add(2 * h + k, k)
            for j in range((TOTAL - 3) // 2 * 2, TOTAL):
                if j + 3 < TOTAL:
                    gather(j + 3, 1 - j % 2)
                add(j, j % 2)
            pool.wait_ge(s_add, 16 * NS)

        @block.scalar
        def _(act):
            def x_hi(j):
                act.wait_ge(s_xT, j + 1)
                wait(act, s_gu, j)
                act.activation(fxT[0][:, :, :], p_x[:, 0:KC * P].rearrange("p (c t) -> p c t", t=P),
                               ACT.Copy).then_inc(s_xhi, 1)

            x_hi(0)

            def step(j, k, shared):
                last = isinstance(j, int) and j == TOTAL - 1
                act.wait_ge(s_gu, j + 1)
                wait(act, s_hid, j)
                act.activation(sil[:, :].rearrange("p (n f) -> p n f", f=FH), p_gu[:, 0:2, 0:FH], ACT.Silu).then_inc(s_sil, 1)
                if not last:
                    x_hi(j + 1)
                if not (isinstance(j, int) and j == 0):
                    send(j - 1, 1 - k, shared if not isinstance(j, int) else j - 1 < NT)
                act.wait_ge(s_hT, j + 1)
                act.activation(hT[0][:, 0:4, :], p_h[:, 0, :].rearrange("p (c t) -> p c t", t=P), ACT.Copy)
                act.activation(hT[0][:, 4:FC, :], p_h[:, 1, 0:2 * P].rearrange("p (c t) -> p c t", t=P),
                               ACT.Copy).then_inc(s_hhi, 1)

            def send(j, k, shared):
                if shared:
                    act.wait_ge(s_yo, j + 1)
                    act.dma_start(tile(o_t, j), yout[k][:, :]).then_inc(s_out[k], 16)
            tiles(act, step)

        @block.vector
        def _(dve):
            nc.vector.memset(hid[:, FF:FC * P], 0.0).then_inc(s_pad, 1)

            def x_lo(j):
                dve.wait_ge(s_xhi, j + 1)
                nc.vector.tensor_tensor(fxT[1][:, :, :], p_x[:, 0:KC * P].rearrange("p (c t) -> p c t", t=P),
                                        fxT[0][:, :, :], ALU.subtract).then_inc(s_xlo, 1)

            def result(j, k, shared):
                dve.wait_ge(s_y, j + 1)
                if shared:
                    half = j // 2
                    wait(dve, s_out[k], 16 * half)
                    dve.wait_ge(s_res[k], 16 * (half + 1))
                    nc.vector.scalar_tensor_tensor(out=yout[k][:, :], in0=p_y[:, 0:H], scalar=tgf[:, :],
                                                   in1=res[k][:, :], op0=ALU.mult, op1=ALU.add).then_inc(s_yo, 1)
                else:
                    if isinstance(j, int) and j < NT + 2:
                        dve.wait_ge(s_out[k], 16 * (NT // 2))
                        dve.wait_ge(s_slots, 16)
                    else:
                        dve.wait_ge(s_add, 16 * (j - NT - 1))
                    nc.vector.tensor_scalar(yout[k][:, :], p_y[:, 0:H], slots[:, bass.ds(j - NT, 1), 1],
                                            None, ALU.mult).then_inc(s_yo, 1)

            x_lo(0)

            def step(j, k, shared):
                last = isinstance(j, int) and j == TOTAL - 1
                dve.wait_ge(s_sil, j + 1)
                wait(dve, s_hT, j)
                nc.vector.tensor_tensor(hid[:, 0:FF].rearrange("p (n f) -> p n f", f=FH), p_gu[:, 2:4, 0:FH],
                                        sil[:, :].rearrange("p (n f) -> p n f", f=FH), ALU.mult).then_inc(s_hid, 1)
                if not last:
                    x_lo(j + 1)
                if not (isinstance(j, int) and j == 0):
                    result(j - 1, 1 - k, shared if not isinstance(j, int) else j - 1 < NT)
                dve.wait_ge(s_hhi, j + 1)
                nc.vector.tensor_tensor(hT[1][:, 0:4, :], p_h[:, 0, :].rearrange("p (c t) -> p c t", t=P),
                                        hT[0][:, 0:4, :], ALU.subtract)
                nc.vector.tensor_tensor(hT[1][:, 4:FC, :], p_h[:, 1, 0:2 * P].rearrange("p (c t) -> p c t", t=P),
                                        hT[0][:, 4:FC, :], ALU.subtract).then_inc(s_hlo, 1)
            tiles(dve, step)
            result(TOTAL - 1, (TOTAL - 1) % 2, False)

        @block.tensor
        def _(pe):
            def x_T(j, k, shared):
                if shared:
                    pe.wait_ge(s_in[k], 16 * (j // 2 + 1))
                else:
                    pe.wait_ge(s_gat[k], 16 * ((j - NT) // 2 + 1))
                wait(pe, s_xlo, j)
                for c in range(KC):
                    last = nc.tensor.transpose(p_x[:, c * P:(c + 1) * P], xin[k][:, c * P:(c + 1) * P], ident[:, :])
                last.then_inc(s_xT, 1)

            def gate_up(j, e):
                pe.wait_ge(s_xlo, j + 1)
                wait(pe, s_hid, j)
                for c in range(KC):
                    for q, (a, b) in enumerate(PASSES):
                        for n in range(4):
                            last = nc.tensor.matmul(p_gu[:, n, 0:FH], fxT[a][:, c, :],
                                                    wgu[b][:, bass.ds(e * KC + c, 1), n * FH:(n + 1) * FH],
                                                    start=(c == 0 and q == 0), stop=(c == KC - 1 and q == 2))
                last.then_inc(s_gu, 1)

            def down(j, e):
                pe.wait_ge(s_hlo, j + 1)
                wait(pe, s_yo, j)
                for c in range(FC):
                    r = min(P, FF - c * P)
                    for q, (a, b) in enumerate(PASSES):
                        last = nc.tensor.matmul(p_y[:, 0:H], hT[a][0:r, c, :], wd[b][0:r, bass.ds(e * FC + c, 1), :],
                                                start=(c == 0 and q == 0), stop=(c == FC - 1 and q == 2))
                last.then_inc(s_y, 1)

            def hidden_T(j):
                pe.wait_ge(s_hid, j + 1)
                wait(pe, s_hlo, j)
                for c in range(FC):
                    last = nc.tensor.transpose(p_h[:, c // 4, (c % 4) * P:(c % 4 + 1) * P], hid[:, c * P:(c + 1) * P],
                                               ident[:, :])
                last.then_inc(s_hT, 1)

            held = [pe.alloc_register(f"expert_of_tile{k}") for k in range(2)]

            def hold(j, k):
                pe.reg_load(held[k], expert_of[0:1, bass.ds(j - NT, 1)])

            def expert(k):
                return pe.snap(held[k], min_val=0, max_val=E - 1)

            pe.wait_ge(s_pad, 1)
            x_T(0, 0, True)

            def step(j, k, shared):
                fixed = isinstance(j, int)
                gate_up(j, E if shared else expert(k))
                if not (fixed and j == TOTAL - 1):
                    x_T(j + 1, 1 - k, shared if not fixed else j + 1 < NT)
                if not (fixed and j == 0):
                    before_shared = shared if not fixed else j - 1 < NT
                    down(j - 1, E if before_shared else expert(1 - k))
                    next_shared = shared if not fixed else j + 1 < NT
                    if not next_shared and not (fixed and j == TOTAL - 1):
                        hold(j + 1, 1 - k)
                hidden_T(j)
            tiles(pe, step)
            down(TOTAL - 1, expert((TOTAL - 1) % 2))


_INS = ['x', 'ctx_1024', 'mask_Bx1xSxS2_if1', 'g_xattn', 'g_ffn', 'L0_xattn_w_q', 'L0_xattn_b_q', 'L0_xattn_w_k',
        'L0_xattn_b_k', 'L0_xattn_w_v', 'L0_xattn_b_v', 'L0_xattn_w_o', 'L0_xattn_b_o', 'L0_ffn_gate_w', 'L0_ffn_eg',
        'L0_ffn_eu', 'L0_ffn_ed', 'L0_ffn_sg', 'L0_ffn_su', 'L0_ffn_sd']


def kernel(**inputs):
    import numpy as _np
    import concourse.bacc as _bacc
    from concourse import mybir as _mybir
    from concourse.bass_utils import run_bass_kernel_spmd as _run

    nc = _bacc.Bacc("TRN2", target_bir_lowering=False, num_devices=1)
    arrays, args = {}, []
    for name in _INS:
        a = _np.ascontiguousarray(inputs[name])
        arrays[f"in_{name}"] = a
        args.append(nc.dram_tensor(f"in_{name}", a.shape, _mybir.dt.from_np(a.dtype), kind="ExternalInput").ap())
    args.append(nc.dram_tensor("out_rows", (N + P, H), _mybir.dt.float32, kind="ExternalOutput").ap())
    flamingo(nc, *args)
    r = _run(nc, [arrays], core_ids=[0])
    return r.results[0]["out_rows"][0:N].reshape(B, S, H)
```
